# Optimizing a Trainium2 kernel written in Bass

```python
import numpy as np
import jax
import jax.numpy as jnp

def _softmax(x, axis=-1):
    return jax.nn.softmax(x, axis=axis)

def _gelu(x):
    return jax.nn.gelu(x, approximate=True)

def _silu(x):
    return jax.nn.silu(x)

def _sigmoid(x):
    return jax.nn.sigmoid(x)

def _layernorm(x, axis=-1, eps=1e-05):
    m = jnp.mean(x, axis=axis, keepdims=True)
    v = jnp.var(x, axis=axis, keepdims=True)
    return (x - m) / jnp.sqrt(v + eps)

def _scatter_add(tgt, idx, src, axis=0):
    return tgt.at[idx].add(src)

def _segment_sum(src, seg, n):
    return jax.ops.segment_sum(src, seg, n)
kernel_name = 'mk_flamingo_gated_d2_seqx_r8_a33581'

def setup_inputs(seed: int=0):
    np.random.seed(seed)
    _w = jnp.asarray

    def _rec_inputs():
        import jax
        import jax.numpy as jnp
        _rk = jax.random.key(seed)
        x = 0.000341 + 1 * jax.random.normal(jax.random.fold_in(_rk, 1), (8, 128, 256), jnp.float32)
        _lenS = 128 - jax.random.randint(jax.random.fold_in(_rk, 7), (8,), 0, max(1, 128 // 4) + 1, jnp.int32)
        _lenS2 = 128 - jax.random.randint(jax.random.fold_in(_rk, 8), (8,), 0, max(1, 128 // 4) + 1, jnp.int32)
        _ctx_2048P = jax.random.normal(jax.random.fold_in(_rk, 11), (8, 16, 256), jnp.float32)
        _ctx_2048c = jax.random.dirichlet(jax.random.fold_in(_rk, 511), 0.3 * jnp.ones((16,), jnp.float32), (8, 128))
        _ctx_2048t = jnp.einsum('bsk,bkd->bsd', _ctx_2048c, _ctx_2048P)
        _ctx_2048t = _ctx_2048t * jax.lax.rsqrt(jnp.mean(jnp.square(_ctx_2048t)) + 1e-12) * 0.953939
        ctx_2048 = -1.47943e-05 + 1.00017 * (_ctx_2048t + 0.3 * jax.random.normal(jax.random.fold_in(_rk, 611), (8, 128, 256), jnp.float32))
        _g = jax.random.normal(jax.random.fold_in(_rk, 9001), (2, 2), jnp.float32)
        _g = jnp.sign(_g) * jnp.maximum(jnp.abs(_g), 1.0) + (_g == 0) * 1.0
        g_xattn = _g[0]
        g_ffn = _g[1]
        return (x, ctx_2048, g_xattn, g_ffn)
    x, ctx_2048, g_xattn, g_ffn = _rec_inputs()

    def _L0_xattn_setup():
        import jax, jax.numpy as jnp
        import numpy as np

        def _wkv(time_decay, time_first, k, v):
            w = -jnp.exp(time_decay)
            u = time_first
            B, T, C = k.shape
            aa = jnp.zeros((B, C), dtype=k.dtype)
            bb = jnp.zeros((B, C), dtype=k.dtype)
            pp = jnp.full((B, C), -1e+38, dtype=k.dtype)

            def step(carry, kv_t):
                aa, bb, pp = carry
                kt, vt = kv_t
                ww = u + kt
                q = jnp.maximum(pp, ww)
                e1 = jnp.exp(pp - q)
                e2 = jnp.exp(ww - q)
                y_t = (e1 * aa + e2 * vt) / (e1 * bb + e2)
                ww2 = pp + w
                q2 = jnp.maximum(ww2, kt)
                e1b = jnp.exp(ww2 - q2)
                e2b = jnp.exp(kt - q2)
                new_carry = (e1b * aa + e2b * vt, e1b * bb + e2b, q2)
                return (new_carry, y_t)
            ks = jnp.transpose(k, (1, 0, 2))
            vs = jnp.transpose(v, (1, 0, 2))
            _, ys = jax.lax.scan(step, (aa, bb, pp), (ks, vs))
            return jnp.transpose(ys, (1, 0, 2))
        key = jax.random.key(seed)
        k1, k2, k3, k4 = jax.random.split(key, 4)
        B, T, C = (8, 128, 256)
        return {'batch_size': B, 'seq_len': T, 'embedding_dim': C, 'time_decay': jax.random.normal(k1, (C,), dtype=jnp.float32), 'time_first': jax.random.normal(k2, (C,), dtype=jnp.float32), 'k': jax.random.normal(k3, (B, T, C), dtype=jnp.float32), 'v': jax.random.normal(k4, (B, T, C), dtype=jnp.float32)}
    _L0_xattn_all = _L0_xattn_setup()
    _L0_xattn_in = {k: v for k, v in _L0_xattn_all.items() if k in ('time_decay', 'time_first')}
    del _L0_xattn_all

    def _L0_ffn_setup():
        import jax, jax.numpy as jnp
        import numpy as np
        B, T, D = (2, 128, 256)
        E, F, K = (64, 64, 4)
        S, HS = (2, 64 * 4)
        key = jax.random.key(seed)
        ks = jax.random.split(key, 9)
        s = 0.02
        f32 = jnp.float32
        return {'x': jax.random.normal(ks[0], (B, T, D), f32), 'router_w': jax.random.normal(ks[1], (D, E), f32) * s, 'router_bias': jnp.zeros((E,), f32), 'wg': jax.random.normal(ks[2], (E, D, F), f32) * s, 'wu': jax.random.normal(ks[3], (E, D, F), f32) * s, 'wd': jax.random.normal(ks[4], (E, F, D), f32) * s, 'swg': jax.random.normal(ks[5], (S, D, HS), f32) * s, 'swu': jax.random.normal(ks[6], (S, D, HS), f32) * s, 'swd': jax.random.normal(ks[7], (S, HS, D), f32) * s}
    _L0_ffn_all = _L0_ffn_setup()
    _L0_ffn_in = {k: v for k, v in _L0_ffn_all.items() if k in ('router_w', 'router_bias', 'wg', 'wu', 'wd', 'swg', 'swu', 'swd')}
    del _L0_ffn_all

    def _L1_xattn_setup():
        import jax, jax.numpy as jnp
        import numpy as np
        DIM = 256
        NH = 16
        HD = DIM // NH
        EPS = 1e-06
        IMG_LEN = 257

        def rms_norm(x, w, eps=EPS):
            xf = x.astype(jnp.float32)
            y = xf * jax.lax.rsqrt(jnp.mean(xf * xf, axis=-1, keepdims=True) + eps)
            return y.astype(x.dtype) * w

        def linear(x, w, b):
            return jnp.einsum('blc,oc->blo', x, w) + b

        def attention(q, k, v):
            scale = 1.0 / jnp.sqrt(jnp.asarray(HD, q.dtype))
            scores = jnp.einsum('bqhd,bkhd->bhqk', q, k) * scale
            probs = jax.nn.softmax(scores, axis=-1)
            return jnp.einsum('bhqk,bkhd->bqhd', probs, v)
        key = jax.random.key(seed)
        ks = jax.random.split(key, 12)
        B, L = (2, 1024)
        s = 0.02
        inp = {'x': jax.random.normal(ks[0], (B, L, DIM), jnp.float32), 'context': jax.random.normal(ks[1], (B, 769, DIM), jnp.float32), 'q_w': jax.random.normal(ks[2], (DIM, DIM), jnp.float32) * s, 'q_b': jnp.zeros((DIM,), jnp.float32), 'k_w': jax.random.normal(ks[3], (DIM, DIM), jnp.float32) * s, 'k_b': jnp.zeros((DIM,), jnp.float32), 'v_w': jax.random.normal(ks[4], (DIM, DIM), jnp.float32) * s, 'v_b': jnp.zeros((DIM,), jnp.float32), 'k_img_w': jax.random.normal(ks[5], (DIM, DIM), jnp.float32) * s, 'k_img_b': jnp.zeros((DIM,), jnp.float32), 'v_img_w': jax.random.normal(ks[6], (DIM, DIM), jnp.float32) * s, 'v_img_b': jnp.zeros((DIM,), jnp.float32), 'o_w': jax.random.normal(ks[7], (DIM, DIM), jnp.float32) * s, 'o_b': jnp.zeros((DIM,), jnp.float32), 'norm_q_w': jnp.ones((DIM,), jnp.float32), 'norm_k_w': jnp.ones((DIM,), jnp.float32), 'norm_k_img_w': jnp.ones((DIM,), jnp.float32)}
        return inp
    _L1_xattn_all = _L1_xattn_setup()
    _L1_xattn_in = {k: v for k, v in _L1_xattn_all.items() if k in ('q_w', 'q_b', 'k_w', 'k_b', 'v_w', 'v_b', 'k_img_w', 'k_img_b', 'v_img_w', 'v_img_b', 'o_w', 'o_b', 'norm_q_w', 'norm_k_w', 'norm_k_img_w')}
    del _L1_xattn_all

    def _L1_ffn_setup():
        import jax, jax.numpy as jnp
        import numpy as np
        _FP8_MAX = 448.0
        _BLOCK = 32
        _EPS = 1e-30

        def _mx_dequant(t):
            rows, feat = t.shape
            blocks = t.reshape(rows, feat // _BLOCK, _BLOCK)
            max_abs = jnp.max(jnp.abs(blocks), axis=-1)
            scales = jnp.maximum(max_abs / _FP8_MAX, _EPS)
            q = (blocks / scales[..., None]).astype(jnp.float8_e4m3fn).astype(jnp.float32)
            return (q * scales[..., None]).reshape(rows, feat)

        def _mx_linear(x2d, w):
            return _mx_dequant(x2d) @ _mx_dequant(w).T
        key = jax.random.key(seed)
        k1, k2, k3, k4 = jax.random.split(key, 4)
        B, S, H, I = (2, 128, 256, 1024)
        return {'x': jax.random.normal(k1, (B, S, H), dtype=jnp.float32), 'gate_w': jax.random.normal(k2, (I, H), dtype=jnp.float32) * 0.02, 'up_w': jax.random.normal(k3, (I, H), dtype=jnp.float32) * 0.02, 'down_w': jax.random.normal(k4, (H, I), dtype=jnp.float32) * 0.02}
    _L1_ffn_all = _L1_ffn_setup()
    _L1_ffn_in = {k: v for k, v in _L1_ffn_all.items() if k in ('gate_w', 'up_w', 'down_w')}
    del _L1_ffn_all
    return {'x': x, 'ctx_2048': ctx_2048, 'g_xattn': g_xattn, 'g_ffn': g_ffn, 'L0_xattn_time_decay': _L0_xattn_in['time_decay'], 'L0_xattn_time_first': _L0_xattn_in['time_first'], 'L0_ffn_router_w': _L0_ffn_in['router_w'], 'L0_ffn_router_bias': _L0_ffn_in['router_bias'], 'L0_ffn_wg': _L0_ffn_in['wg'], 'L0_ffn_wu': _L0_ffn_in['wu'], 'L0_ffn_wd': _L0_ffn_in['wd'], 'L0_ffn_swg': _L0_ffn_in['swg'], 'L0_ffn_swu': _L0_ffn_in['swu'], 'L0_ffn_swd': _L0_ffn_in['swd'], 'L1_xattn_q_w': _L1_xattn_in['q_w'], 'L1_xattn_q_b': _L1_xattn_in['q_b'], 'L1_xattn_k_w': _L1_xattn_in['k_w'], 'L1_xattn_k_b': _L1_xattn_in['k_b'], 'L1_xattn_v_w': _L1_xattn_in['v_w'], 'L1_xattn_v_b': _L1_xattn_in['v_b'], 'L1_xattn_k_img_w': _L1_xattn_in['k_img_w'], 'L1_xattn_k_img_b': _L1_xattn_in['k_img_b'], 'L1_xattn_v_img_w': _L1_xattn_in['v_img_w'], 'L1_xattn_v_img_b': _L1_xattn_in['v_img_b'], 'L1_xattn_o_w': _L1_xattn_in['o_w'], 'L1_xattn_o_b': _L1_xattn_in['o_b'], 'L1_xattn_norm_q_w': _L1_xattn_in['norm_q_w'], 'L1_xattn_norm_k_w': _L1_xattn_in['norm_k_w'], 'L1_xattn_norm_k_img_w': _L1_xattn_in['norm_k_img_w'], 'L1_ffn_gate_w': _L1_ffn_in['gate_w'], 'L1_ffn_up_w': _L1_ffn_in['up_w'], 'L1_ffn_down_w': _L1_ffn_in['down_w']}

def reference(x, ctx_2048, g_xattn, g_ffn, L0_xattn_time_decay, L0_xattn_time_first, L0_ffn_router_w, L0_ffn_router_bias, L0_ffn_wg, L0_ffn_wu, L0_ffn_wd, L0_ffn_swg, L0_ffn_swu, L0_ffn_swd, L1_xattn_q_w, L1_xattn_q_b, L1_xattn_k_w, L1_xattn_k_b, L1_xattn_v_w, L1_xattn_v_b, L1_xattn_k_img_w, L1_xattn_k_img_b, L1_xattn_v_img_w, L1_xattn_v_img_b, L1_xattn_o_w, L1_xattn_o_b, L1_xattn_norm_q_w, L1_xattn_norm_k_w, L1_xattn_norm_k_img_w, L1_ffn_gate_w, L1_ffn_up_w, L1_ffn_down_w):
    import jax
    import jax.numpy as jnp

    def _L0_xattn_ref(batch_size, seq_len, embedding_dim, time_decay, time_first, k, v):
        import jax, jax.numpy as jnp
        import numpy as np

        def _wkv(time_decay, time_first, k, v):
            w = -jnp.exp(time_decay)
            u = time_first
            B, T, C = k.shape
            aa = jnp.zeros((B, C), dtype=k.dtype)
            bb = jnp.zeros((B, C), dtype=k.dtype)
            pp = jnp.full((B, C), -1e+38, dtype=k.dtype)

            def step(carry, kv_t):
                aa, bb, pp = carry
                kt, vt = kv_t
                ww = u + kt
                q = jnp.maximum(pp, ww)
                e1 = jnp.exp(pp - q)
                e2 = jnp.exp(ww - q)
                y_t = (e1 * aa + e2 * vt) / (e1 * bb + e2)
                ww2 = pp + w
                q2 = jnp.maximum(ww2, kt)
                e1b = jnp.exp(ww2 - q2)
                e2b = jnp.exp(kt - q2)
                new_carry = (e1b * aa + e2b * vt, e1b * bb + e2b, q2)
                return (new_carry, y_t)
            ks = jnp.transpose(k, (1, 0, 2))
            vs = jnp.transpose(v, (1, 0, 2))
            _, ys = jax.lax.scan(step, (aa, bb, pp), (ks, vs))
            return jnp.transpose(ys, (1, 0, 2))
        assert seq_len <= 128
        return _wkv(time_decay, time_first, k, v)

    def _L0_ffn_ref(x, router_w, router_bias, wg, wu, wd, swg, swu, swd):
        import jax, jax.numpy as jnp
        import numpy as np
        B, T, D = (2, 128, 256)
        E, F, K = (64, 64, 4)
        S, HS = (2, 64 * 4)
        b, t, d = x.shape
        flat = x.reshape(b * t, d)
        n = flat.shape[0]
        logits = flat @ router_w
        scores = jax.nn.softmax(logits, axis=-1)
        _, topk_idx = jax.lax.top_k(logits + router_bias, K)
        topk_scores = jnp.take_along_axis(scores, topk_idx, axis=-1)
        topk_scores = topk_scores / topk_scores.sum(axis=-1, keepdims=True)
        comb = jnp.zeros((n, E), dtype=flat.dtype).at[jnp.arange(n)[:, None], topk_idx].set(topk_scores)
        g = jax.nn.silu(jnp.einsum('nd,edf->nef', flat, wg))
        u = jnp.einsum('nd,edf->nef', flat, wu)
        routed = jnp.einsum('ne,nef,efd->nd', comb, g * u, wd)
        sg = jax.nn.silu(jnp.einsum('nd,sdh->nsh', flat, swg))
        su = jnp.einsum('nd,sdh->nsh', flat, swu)
        shared = jnp.einsum('nsh,shd->nd', sg * su, swd)
        return (routed + shared).reshape(b, t, d)

    def _L1_xattn_ref(x, context, q_w, q_b, k_w, k_b, v_w, v_b, k_img_w, k_img_b, v_img_w, v_img_b, o_w, o_b, norm_q_w, norm_k_w, norm_k_img_w):
        import jax, jax.numpy as jnp
        import numpy as np
        DIM = 256
        NH = 16
        HD = DIM // NH
        EPS = 1e-06
        IMG_LEN = 257

        def rms_norm(x, w, eps=EPS):
            xf = x.astype(jnp.float32)
            y = xf * jax.lax.rsqrt(jnp.mean(xf * xf, axis=-1, keepdims=True) + eps)
            return y.astype(x.dtype) * w

        def linear(x, w, b):
            return jnp.einsum('blc,oc->blo', x, w) + b

        def attention(q, k, v):
            scale = 1.0 / jnp.sqrt(jnp.asarray(HD, q.dtype))
            scores = jnp.einsum('bqhd,bkhd->bhqk', q, k) * scale
            probs = jax.nn.softmax(scores, axis=-1)
            return jnp.einsum('bhqk,bkhd->bqhd', probs, v)
        B, L, _ = x.shape
        ctx_img = context[:, :IMG_LEN]
        ctx_txt = context[:, IMG_LEN:]
        q = rms_norm(linear(x, q_w, q_b), norm_q_w).reshape(B, L, NH, HD)
        k = rms_norm(linear(ctx_txt, k_w, k_b), norm_k_w).reshape(B, -1, NH, HD)
        v = linear(ctx_txt, v_w, v_b).reshape(B, -1, NH, HD)
        k_img = rms_norm(linear(ctx_img, k_img_w, k_img_b), norm_k_img_w).reshape(B, -1, NH, HD)
        v_img = linear(ctx_img, v_img_w, v_img_b).reshape(B, -1, NH, HD)
        img_x = attention(q, k_img, v_img)
        txt_x = attention(q, k, v)
        out = (txt_x + img_x).reshape(B, L, DIM)
        return linear(out, o_w, o_b)

    def _L1_ffn_ref(x, gate_w, up_w, down_w):
        import jax, jax.numpy as jnp
        import numpy as np
        _FP8_MAX = 448.0
        _BLOCK = 32
        _EPS = 1e-30

        def _mx_dequant(t):
            rows, feat = t.shape
            blocks = t.reshape(rows, feat // _BLOCK, _BLOCK)
            max_abs = jnp.max(jnp.abs(blocks), axis=-1)
            scales = jnp.maximum(max_abs / _FP8_MAX, _EPS)
            q = (blocks / scales[..., None]).astype(jnp.float8_e4m3fn).astype(jnp.float32)
            return (q * scales[..., None]).reshape(rows, feat)

        def _mx_linear(x2d, w):
            return _mx_dequant(x2d) @ _mx_dequant(w).T
        B, S, H = x.shape
        x2d = x.reshape(B * S, H)
        gate = _mx_linear(x2d, gate_w)
        up = _mx_linear(x2d, up_w)
        h = jax.nn.silu(gate) * up
        out = _mx_linear(h, down_w)
        return out.reshape(B, S, H)
    x = x + jnp.tanh(g_xattn[0]) * _L0_xattn_ref(8, 128, 256, L0_xattn_time_decay, L0_xattn_time_first, _layernorm(x, axis=-1), ctx_2048)
    x = x + jnp.tanh(g_ffn[0]) * _L0_ffn_ref(_layernorm(x, axis=-1), L0_ffn_router_w, L0_ffn_router_bias, L0_ffn_wg, L0_ffn_wu, L0_ffn_wd, L0_ffn_swg, L0_ffn_swu, L0_ffn_swd)
    x = x + jnp.tanh(g_xattn[1]) * _L1_xattn_ref(_layernorm(x, axis=-1), ctx_2048, L1_xattn_q_w, L1_xattn_q_b, L1_xattn_k_w, L1_xattn_k_b, L1_xattn_v_w, L1_xattn_v_b, L1_xattn_k_img_w, L1_xattn_k_img_b, L1_xattn_v_img_w, L1_xattn_v_img_b, L1_xattn_o_w, L1_xattn_o_b, L1_xattn_norm_q_w, L1_xattn_norm_k_w, L1_xattn_norm_k_img_w)
    x = x + jnp.tanh(g_ffn[1]) * _L1_ffn_ref(_layernorm(x, axis=-1), L1_ffn_gate_w, L1_ffn_up_w, L1_ffn_down_w)
    return x

_drawn_inputs = setup_inputs


def setup_inputs(seed=0):
    import zlib

    import numpy as np

    out = dict(_drawn_inputs(seed))
    spreads = {'g_ffn': (-1.0, 0.6),
     'L0_ffn_router_bias': (0.0, 0.8),
     'L1_xattn_q_b': (0.0, 2.0),
     'L1_xattn_k_b': (0.0, 0.1),
     'L1_xattn_v_b': (0.0, 0.1),
     'L1_xattn_k_img_b': (0.0, 2.0),
     'L1_xattn_v_img_b': (0.0, 0.936),
     'L1_xattn_o_b': (0.0, 0.297),
     'L1_xattn_norm_q_w': (1.0, 0.6),
     'L1_xattn_norm_k_w': (1.0, 0.2),
     'L1_xattn_norm_k_img_w': (1.0, 0.6)}
    factors = {'L0_ffn_router_w': 8.0,
     'L0_ffn_wg': 8.0,
     'L0_ffn_wu': 8.0,
     'L0_ffn_wd': 8.0,
     'L0_ffn_swg': 3.689,
     'L0_ffn_swu': 3.617,
     'L0_ffn_swd': 3.636,
     'L1_xattn_q_w': 28.815,
     'L1_xattn_k_img_w': 22.042,
     'L1_xattn_v_img_w': 3.354,
     'L1_ffn_gate_w': 6.016,
     'L1_ffn_up_w': 5.895,
     'L1_ffn_down_w': 5.899}
    for name, (base, spread) in spreads.items():
        noise = np.random.default_rng([zlib.crc32(name.encode()), seed]).standard_normal(out[name].shape)
        drawn = base * np.exp(spread * noise) if base else spread * noise
        out[name] = jnp.asarray(drawn.astype(out[name].dtype))
    for name, factor in factors.items():
        out[name] = (out[name] * factor).astype(out[name].dtype)
    return out
```

```python
from contextlib import ExitStack

import concourse.bass as bass
from concourse import mybir

ALU = mybir.AluOpType
ACT = mybir.ActivationFunctionType
AX = mybir.AxisListType
F32 = mybir.dt.float32
F16 = mybir.dt.float16
BF16 = mybir.dt.bfloat16
I32 = mybir.dt.int32
U32 = mybir.dt.uint32

P = 128
D = 256
C = D // P
T = 8
N = T * P
E = 64
F = 64
K = 4
NB = 96
SH = 512
H = 16
HD = D // H
HP = 32
INNER = 1024
QB = 32
LN_EPS = 1e-5
RMS_EPS = 1e-6
FP8_MAX = 448.0
FP8_TINY = 2.0 ** -6
ROUND4 = 1.5 * 2.0 ** 20
EXPONENT = 0x7F800000


class Item:

    def __init__(self, n, slot, lap):
        self.n, self.slot, self.lap = n, slot, lap


def run_steps(eng, items, depth, unroll, body, lead=1, tail=0):

    def step(g, k):
        def at(d=0, slots=unroll):
            lap, slot = (k - d) // unroll, (k - d) % unroll
            n = g * unroll + (k - d)
            if isinstance(g, int) and not 0 <= n < items:
                return None
            per = unroll // slots
            return Item(n, slot % slots, (g + lap) * per + slot // slots)
        body(at)

    whole = (items - tail) // unroll
    lead = min(lead, whole)
    for s in range(lead * unroll):
        step(s // unroll, s % unroll)
    if whole > lead:
        with eng.Fori(lead, whole) as g:
            for k in range(unroll):
                step(g, k)
    for s in range(whole * unroll, items + depth):
        step(s // unroll, s % unroll)


def reach(eng, sem, value):
    if isinstance(value, int) and value <= 0:
        return
    eng.wait_ge(sem, value)


def wait_apart(eng, met, *waits):
    waits = [(s, v if isinstance(v, int) else eng.to_reg(v)) for s, v in waits
             if not (isinstance(v, int) and v <= 0)]
    eng.wait_ge(*met)
    for s, v in waits:
        eng.wait_ge(s, v)


def build_program(nc, x, ctx_in, g_xattn, g_ffn, time_decay, time_first, router_w, router_bias,
                  wg, wu, wd, swg, swu, swd, q_w, q_b, k_w, k_b, v_w, v_b, o_w, o_b,
                  norm_q_w, norm_k_w, gate_w, up_w, down_w, out):
    h1_dram = nc.dram_tensor("h1_dram", (N, D), F32, kind="Internal").ap()
    ys_dram = nc.dram_tensor("ys_dram", (NB * P, D), F32, kind="Internal").ap()

    with ExitStack() as ctx:
        def sb(name, shape, dt=F32):
            return ctx.enter_context(nc.sbuf_tensor(name, shape, dt))

        sems = {}

        def sem(name):
            if name not in sems:
                sems[name] = ctx.enter_context(nc.semaphore(name))
            return sems[name]

        bank = [ctx.enter_context(nc.psum_tensor(f"bank{i}", [P, 512], F32)) for i in range(8)]

        arena_up = sb("arena_up", [P, C * E * 2 * F])
        arena_dn = sb("arena_dn", [P, E * D])
        moe_up = arena_up[:, :].rearrange("p (c e f) -> p c e f", c=C, e=E)
        moe_dn = arena_dn[0:F, :].rearrange("p (e d) -> p e d", e=E)
        x_res = sb("x_res", [P, T, D])
        h1T = sb("h1T", [P, C, N])
        shared = sb("shared", [P, 3072])
        sgu_w = shared[:, 0:2048].rearrange("p (c n) -> p c n", c=C)
        sd_w = shared[:, 2048:3072].rearrange("p (f n) -> p f n", f=SH // P)
        attn_w = sb("attn_w", [P, 4, C, D])
        mx_w = sb("mx_w", [P, 6144])
        mx_gu = mx_w[:, 0:4096].rearrange("p (c n) -> p c n", c=C)
        mx_dn = mx_w[:, 4096:6144].rearrange("p (i n) -> p i n", i=INNER // P)
        w_nat = mx_w[:, 0:2048].rearrange("p (w o n) -> p w o n", w=4, o=C)
        hs = mx_w[:, 0:4096].rearrange("p (f n) -> p f n", f=SH // P)
        router_sb = sb("router_sb", [P, C, E])
        rbias = sb("rbias", [P, E])
        bias_bc = sb("bias_bc", [P, 6, D])
        QB_, KB_, VB_, OB_, NQ_, NK_ = range(6)
        gates = sb("gates", [P, 4])
        tg = sb("tg", [P, 4])
        GX0, GX1, GF0, GF1 = range(4)
        ident = sb("ident", [P, P])
        tri = sb("tri", [P, P], BF16)
        ones = sb("ones", [P, P], BF16)
        iota = sb("iota", [P, P])
        pcol = sb("pcol", [P, 1])
        tokid = sb("tokid", [P, T])
        mhalf = sb("mhalf", [P, T])
        decay = sb("decay", [P, C])
        wdec = sb("wdec", [P, C])
        tdtf = sb("tdtf", [P, 2, C])
        negm = sb("negm", [P, C])
        umm = sb("umm", [P, C])
        stats = sb("stats", [P, T, 6])
        mv = sb("mv", [P, T, 2])
        rstd = sb("rstd", [P, T])
        macc = sb("macc", [P, 2, E], BF16)
        combs = sb("combs", [P, T, K])
        rank_all = sb("rank_all", [P, T, K])
        slot_u = sb("slot_u", [P, T * K], U32)
        tokf = sb("tokf", [P, NB])
        eid_row = sb("eid_row", [1, P], I32)

        def carver(region, at=0):
            state = [at]

            def take(*shape, dt=F32):
                n = 1
                for s in shape:
                    n *= s
                words = (n + 1) // 2 if dt in (F16, BF16) else n
                words = (words + 7) // 8 * 8
                a = region[:, state[0]:state[0] + words]
                state[0] += words
                assert state[0] <= region.shape[1], state[0]
                if dt != F32:
                    a = a.bitcast(dt)
                a = a[:, 0:n]
                if len(shape) == 1:
                    return a
                names = "abcd"[:len(shape)]
                return a.rearrange(f"p ({' '.join(names)}) -> p {' '.join(names)}",
                                   **dict(zip(names[:-1], shape)))
            return take

        take = carver(arena_dn, E * D // 2)
        A = 2
        xnA = [take(D) for _ in range(A)]
        cxA = [take(D) for _ in range(A)]
        ekm = [take(C, P) for _ in range(A)]
        eku = [take(C, P) for _ in range(A)]
        vTs = [take(C, P) for _ in range(A)]
        pm = [take(C, P) for _ in range(A)]
        pu = [take(C, P) for _ in range(A)]
        sA = [take(C, P + 1) for _ in range(A)]
        sB = [take(C, P + 1) for _ in range(A)]
        num = [take(C, P) for _ in range(A)]
        den = [take(C, P) for _ in range(A)]
        yA = [take(C, P) for _ in range(A)]

        take = carver(arena_dn, E * D // 2)
        onehot = take(T, K, E, dt=BF16)
        tmp = take(T * K, E)
        sgt = [take(512) for _ in range(2)]
        upt = [take(512) for _ in range(2)]
        h1B = [take(D) for _ in range(2)]
        h1Ts = [take(C, P) for _ in range(2)]
        biased = [take(E) for _ in range(2)]
        pexp = [take(E) for _ in range(2)]
        mask = [take(E, dt=BF16) for _ in range(2)]
        nmx = [take(1) for _ in range(2)]
        v8 = take(8)
        i8 = take(8, dt=U32)
        i8f = take(8)
        ck = take(K)
        cs = take(1)
        rcs = take(1)
        prod = take(K, E)
        prod2 = take(K, E)
        cnt_i = take(E, dt=I32)
        nb_i = take(E, dt=I32)
        nbf = take(E)
        cum = take(E)
        base = take(E)
        cmp = take(E)
        eidf = take(1)
        eidm = take(1)
        sbase = take(T * K)
        slotf = take(T * K)
        slot_i = take(T * K, dt=I32)
        blk_i = take(T * K, dt=I32)
        pos_i = take(T * K, dt=I32)
        blkf = take(T * K)
        posf = take(T * K)
        poh = [take(P, dt=F16) for _ in range(4)]
        boh = [take(NB, dt=F16) for _ in range(4)]

        take = carver(shared)
        xg = [take(D) for _ in range(4)]
        xgT = [take(C, P) for _ in range(2)]
        sgb = [take(F) for _ in range(2)]
        hb = [take(F) for _ in range(2)]
        hbT = [take(P) for _ in range(2)]
        ysb = [take(D) for _ in range(2)]
        gidx = sb("gidx", [P, 4], U32)

        take = carver(arena_up)
        yk = [[take(D) for _ in range(K)] for _ in range(2)]
        xnE = [take(D) for _ in range(2)]
        cxE = [take(D) for _ in range(2)]
        xTE = [take(C, P) for _ in range(2)]
        cTE = [take(C, P) for _ in range(2)]
        qb = [take(D) for _ in range(2)]
        kb = [take(D) for _ in range(2)]
        sq = [take(D) for _ in range(2)]
        ssq = [take(2) for _ in range(2)]
        rq = [take(2) for _ in range(2)]
        qn = [take(H, HP) for _ in range(2)]
        kn = [take(H, HP) for _ in range(2)]
        qT = [take(4, P) for _ in range(2)]
        kT = [take(4, P) for _ in range(2)]
        va = [take(H, HD + 1) for _ in range(2)]
        smax = [take(H) for _ in range(2)]
        sS = take(4, 4, P)
        pT = take(4, 4, P)
        rsum = [take(H) for _ in range(2)]
        oE = [take(H, HD) for _ in range(2)]
        oT = [take(C, P) for _ in range(2)]
        gob = take(D)

        take = carver(arena_dn)
        xnF = [take(D) for _ in range(2)]
        xyF = take(D)
        xeF = take(D)
        xaF = take(D)
        xqF = [take(D) for _ in range(2)]
        xTF = [take(C, P) for _ in range(2)]
        amx = take(8)
        amc = take(8)
        arc = take(8)
        amh = take(32)
        ahc = take(32)
        ahr = take(32)
        sgF = take(INNER)
        hF = take(INNER)
        heF = take(INNER)
        haF = take(INNER)
        hqF = [take(INNER) for _ in range(2)]
        hTF = [take(8, P) for _ in range(2)]
        wn = [take(1024) for _ in range(2)]
        we, wa = heF, haF
        wq = [take(1024) for _ in range(2)]
        wam = take(32)
        wac = take(32)
        war = take(32)

        small = sb("small", [P, 16])
        epsc = sb("epsc", [P, 2])
        epsr = sb("epsr", [P, 2])
        eidx = sb("eidx", [P, 8], U32)

        gate_v = gate_w.rearrange("(n p) d -> p n d", p=P)
        up_v = up_w.rearrange("(n p) d -> p n d", p=P)
        down_v = down_w.rearrange("(n p) d -> p n d", p=P)

        block = ctx.enter_context(nc.Block())

        @block.sync
        def _(sp):
            def cxA_load(at):
                i = at(0)
                reach(sp, sem("kvT"), i.n - 1)
                sp.dma_start(cxA[i.slot], ctx_in[i.n]).then_inc(sem(f"cxA_in{i.slot}"), 16)

            sp.dma_start(x_res[:, :, :], x.rearrange("t p d -> p t d")).then_inc(sem("x_in"), 16)
            small_in = [(tdtf[:, 0, :], time_decay.rearrange("(c p) -> p c", p=P)),
                        (tdtf[:, 1, :], time_first.rearrange("(c p) -> p c", p=P)),
                        (gates[:, 0:2], g_xattn.partition_broadcast(P)),
                        (gates[:, 2:4], g_ffn.partition_broadcast(P)),
                        (router_sb[:, :, :], router_w.rearrange("(c p) e -> p c e", p=P)),
                        (rbias[:, :], router_bias.partition_broadcast(P))]
            small_in += [(bias_bc[:, n, :], v.partition_broadcast(P))
                         for n, v in enumerate((q_b, k_b, v_b, o_b, norm_q_w, norm_k_w))]
            for dst, src in small_in:
                sp.dma_start(dst, src, allow_slow_non_contiguous=True).then_inc(sem("small_in"), 16)
            for n, w in enumerate((q_w, k_w, v_w, o_w)):
                sp.dma_start(w_nat[:, n, :, :], w.rearrange("(o p) n -> p o n", p=P)).then_inc(sem("wnat_in"), 16)
            run_steps(sp, T, 0, 2, cxA_load)
            for s in range(2):
                for k, w in enumerate((swg, swu)):
                    sp.dma_start(sgu_w[:, :, k * SH + s * D:k * SH + (s + 1) * D],
                                 w[s].rearrange("(c p) n -> p c n", p=P)).then_inc(sem("shared_in"), 16)
                sp.dma_start(sd_w[:, 2 * s:2 * s + 2, :],
                             swd[s].rearrange("(f p) n -> p f n", p=P)).then_inc(sem("shared_in"), 16)
            for c in range(C):
                for n, w in enumerate((wg, wu)):
                    for e in range(0, E, 16):
                        sp.dma_start(moe_up[:, c, e:e + 16, n * F:(n + 1) * F],
                                     w[e:e + 16, c * P:(c + 1) * P, :].rearrange("e p f -> p e f"))\
                          .then_inc(sem("moe_in"), 16)
            for e in range(0, E // 2, 16):
                sp.dma_start(moe_dn[:, e:e + 16, :], wd[e:e + 16].rearrange("e f d -> f e d"))\
                  .then_inc(sem("moe_in"), 16)

            def h1_store(at):
                i = at(0)
                sp.wait_ge(sem("h1"), i.n + 1)
                sp.dma_start(h1_dram[bass.ds(i.n * P, P), :], h1B[i.slot]).then_inc(sem(f"h1_out{i.slot}"), 16)
            run_steps(sp, T, 0, 2, h1_store)
            sp.wait_ge(sem("tok"), 1)
            for b in range(2):
                sp.wait_ge(sem(f"h1_out{b}"), 16 * (T // 2))
            sp.wait_ge(sem("hs"), 8)
            for e in range(E // 2, E, 16):
                sp.dma_start(moe_dn[:, e:e + 16, :], wd[e:e + 16].rearrange("e f d -> f e d"))\
                  .then_inc(sem("moe_in2"), 16)

            def ys_store(at):
                i = at(0, 2)
                sp.wait_ge(sem("ysb"), i.n + 1)
                sp.dma_start(ys_dram[bass.ds(i.n * P, P), :], ysb[i.slot]).then_inc(sem(f"ys_out{i.slot}"), 16)
            run_steps(sp, NB, 0, 4, ys_store)
            sp.wait_ge(sem("gu"), NB)

            def cxE_load(at):
                i = at(0)
                if not (isinstance(i.n, int) and i.n < 2):
                    sp.wait_ge(sem("cTE_ps"), i.n - 1)
                sp.dma_start(cxE[i.slot], ctx_in[i.n]).then_inc(sem(f"cxE_in{i.slot}"), 16)
            run_steps(sp, T, 0, 2, cxE_load)
            sp.wait_ge(sem("mo_y"), NB)
            pieces = [gate_v[:, 4 * n:4 * n + 4, :] for n in range(2)]
            pieces += [up_v[:, 4 * n:4 * n + 4, :] for n in range(2)]
            pieces += [down_v[:, n, :] for n in range(2)]
            for n, src in enumerate(pieces):
                if n >= 2:
                    sp.wait_ge(sem("w_deq"), n - 1)
                dst = wn[n % 2]
                if n < 4:
                    dst = dst.rearrange("p (a b) -> p a b", a=4)
                sp.dma_start(dst, src).then_inc(sem(f"wn_in{n % 2}"), 16)

            def out_store(at):
                i = at(0)
                sp.wait_ge(sem("x4"), i.n + 1)
                sp.dma_start(out[i.n], x_res[:, i.n, :]).then_inc(sem("out_done"), 16)
            run_steps(sp, T, 0, 2, out_store)
            sp.wait_ge(sem("out_done"), 16 * T)

        @block.gpsimd
        def _(pool):
            pool.memset(ident[:, :], 0.0).then_inc(sem("cz"), 1)
            pool.memset(tri[:, :], 1.0).then_inc(sem("cz"), 1)
            pool.memset(ones[:, :], 1.0).then_inc(sem("const"), 1)
            pool.memset(mhalf[:, :], -0.5).then_inc(sem("const"), 1)
            pool.memset(epsc[:, :], LN_EPS).then_inc(sem("const"), 1)
            pool.memset(epsr[:, :], D * RMS_EPS).then_inc(sem("const"), 1)
            pool.memset(macc[:, 0, :], 0.0).then_inc(sem("const"), 1)
            pool.iota(iota[:, :], [[1, P]], base=0, channel_multiplier=0,
                      allow_small_or_imprecise_dtypes=True).then_inc(sem("const"), 1)
            pool.iota(pcol[:, :], [[0, 1]], base=0, channel_multiplier=1,
                      allow_small_or_imprecise_dtypes=True).then_inc(sem("const"), 1)
            pool.iota(tokid[:, :], [[P, T]], base=0, channel_multiplier=1,
                      allow_small_or_imprecise_dtypes=True).then_inc(sem("const"), 1)
            for b in range(A):
                for s in (sA, sB):
                    pool.memset(s[b][:, :, 0:1], 0.0).then_inc(sem("const"), 1)
            pool.wait_ge(sem("cz"), 2)
            pool.affine_select(out=ident[:, :], in_=ident[:, :], compare_op=ALU.not_equal, fill=1.0,
                               base=0, pattern=[[-1, P]], channel_multiplier=1).then_inc(sem("const"), 1)
            pool.affine_select(out=tri[:, :], in_=tri[:, :], compare_op=ALU.is_gt, fill=0.0,
                               base=0, pattern=[[1, P]], channel_multiplier=-1).then_inc(sem("const"), 1)
            CONST = 14

            def inv_sqrt(dst, src, scale, eps, temp, ready, value, done):
                pool.wait_ge(sem(ready), value)
                pool.tensor_scalar(temp, src, scale, eps, ALU.mult, ALU.add).then_inc(sem("isq"), 1)
                isq[0] = isq[0] + 1
                pool.wait_ge(sem("isq"), isq[0])
                pool.tensor_tensor(dst, temp, mhalf[:, 0:temp.shape[1]], ALU.pow).then_inc(sem(done), 1)

            isq = [0]
            pool.wait_ge(sem("const"), CONST)
            inv_sqrt(rstd[:, :], mv[:, :, 1], 1.0, LN_EPS, small[:, 0:T], "mv", T, "rstd")

            def wkv_sums(at):
                i = at(0)
                if i is None:
                    return
                n = i.n
                pool.wait_ge(sem("exps"), n + 1)
                pool.wait_ge(sem("vTs"), n + 1)
                reach(pool, sem("yA"), n - 1)
                pool.tensor_tensor(pu[i.slot], eku[i.slot], vTs[i.slot], ALU.mult).then_inc(sem("pu"), 1)
                pool.wait_ge(sem("scan"), n + 1)
                pool.tensor_tensor(den[i.slot], sB[i.slot][:, :, 0:P], eku[i.slot], ALU.add)
                pool.wait_ge(sem("pu"), n + 1)
                pool.tensor_tensor(num[i.slot], sA[i.slot][:, :, 0:P], pu[i.slot], ALU.add)\
                    .then_inc(sem("numden"), 1)
            run_steps(pool, T, 0, 2, wkv_sums)

            def route_pool(at):
                i = at(0)
                if i is not None:
                    pool.wait_ge(sem("mvB"), i.n + 1)
                    pool.tensor_tensor(small[:, 8 + i.slot:9 + i.slot], mv[:, i.slot, 1:2], epsc[:, 0:1], ALU.add).then_inc(sem("isqB"), 1)
                    pool.wait_ge(sem("isqB"), i.n + 1)
                    pool.tensor_tensor(rstd[:, i.slot:i.slot + 1], small[:, 8 + i.slot:9 + i.slot],
                                       mhalf[:, 0:1], ALU.pow).then_inc(sem("rstdB"), 1)
                i = at(1)
                if i is not None:
                    pool.wait_ge(sem("h1T"), i.n + 1)
                    pool.tensor_copy(h1T[:, :, bass.ds(i.n * P, P)], h1Ts[i.slot]).then_inc(sem("h1T_all"), 1)
                i = at(2)
                if i is not None:
                    pool.wait_ge(sem("mask"), i.n + 1)
                    reach(pool, sem("rank"), i.n)
                    reach(pool, sem("macc"), i.n)
                    pool.tensor_tensor(macc[:, 1 - i.slot, :], macc[:, i.slot, :], mask[i.slot], ALU.add)\
                        .then_inc(sem("macc"), 1)
            run_steps(pool, T, 2, 2, route_pool, lead=2)

            for n in range(8):
                f, hf = n % 4, n // 4
                pool.wait_ge(sem("sgt"), n + 1)
                pool.tensor_tensor(hs[:, f, hf * 512:(hf + 1) * 512], sgt[n % 2], upt[n % 2], ALU.mult)\
                    .then_inc(sem("hs"), 1)

            pool.wait_ge(sem("tok"), 1)
            for b in range(2):
                pool.wait_ge(sem(f"h1_out{b}"), 16 * (T // 2))
            pool.wait_ge(sem("sdown"), 8)

            def gather(at):
                i = at(0)
                if not (isinstance(i.n, int) and i.n < 4):
                    pool.wait_ge(sem("xgT_ps"), i.n - 3)
                pool.tensor_copy(gidx[:, i.slot:i.slot + 1], tokf[:, bass.ds(i.n, 1)]).then_inc(sem("gidx"), 1)
                wait_apart(pool, (sem("tok"), 1), (sem("gidx"), i.n + 1))
                pool.indirect_dma_start(out=xg[i.slot], out_offset=None, in_=h1_dram[:, :],
                                        in_offset=bass.IndirectOffsetOnAxis(ap=gidx[:, i.slot:i.slot + 1], axis=0))\
                    .then_inc(sem(f"xg{i.slot}"), 16)
            run_steps(pool, NB, 0, 4, gather)

            for b in range(2):
                pool.wait_ge(sem(f"ys_out{b}"), 16 * (NB // 2))
            pool.wait_ge(sem("gu"), NB)
            for b in range(2):
                pool.memset(qn[b][:, :, HD:HP], 0.0).then_inc(sem("padE"), 1)
                pool.memset(kn[b][:, :, HD:HP], 0.0).then_inc(sem("padE"), 1)
                pool.memset(va[b][:, :, HD:HD + 1], 1.0).then_inc(sem("padE"), 1)

            def combine(at):
                i = at(0)
                if i is not None:
                    if not (isinstance(i.n, int) and i.n < 2):
                        pool.wait_ge(sem("x2"), i.n - 1)
                    pool.tensor_copy(eidx[:, 4 * i.slot:4 * i.slot + 4], slot_u[:, bass.ds(i.n * K, K)])\
                        .then_inc(sem("eidx"), 1)
                    wait_apart(pool, (sem("tok"), 1), (sem("eidx"), i.n + 1))
                    for k in range(K):
                        pool.indirect_dma_start(
                            out=yk[i.slot][k], out_offset=None, in_=ys_dram[:, :],
                            in_offset=bass.IndirectOffsetOnAxis(ap=eidx[:, 4 * i.slot + k:4 * i.slot + k + 1], axis=0))\
                            .then_inc(sem(f"yk{i.slot}"), 16)
                i = at(1)
                if i is not None:
                    s = i.slot
                    pool.wait_ge(sem("mvE"), i.n + 1)
                    pool.tensor_tensor(small[:, s:s + 1], mv[:, s, 1:2], epsc[:, 0:1], ALU.add)\
                        .then_inc(sem("isqE"), 1)
                    pool.wait_ge(sem("isqE"), i.n + 1)
                    pool.tensor_tensor(rstd[:, s:s + 1], small[:, s:s + 1], mhalf[:, 0:1], ALU.pow)\
                        .then_inc(sem("rstdE"), 1)
                    pool.wait_ge(sem("ssq"), i.n + 1)
                    pool.tensor_tensor(small[:, 4 + 2 * s:6 + 2 * s], ssq[s], epsr[:, :], ALU.add)\
                        .then_inc(sem("isqQ"), 1)
                    pool.wait_ge(sem("isqQ"), i.n + 1)
                    pool.tensor_tensor(rq[s], small[:, 4 + 2 * s:6 + 2 * s], mhalf[:, 0:2], ALU.pow)\
                        .then_inc(sem("rq"), 1)
            run_steps(pool, T, 1, 2, combine)

            def norm_f(at):
                i = at(0)
                s = i.slot
                pool.wait_ge(sem("mvF"), i.n + 1)
                pool.tensor_tensor(small[:, s:s + 1], mv[:, s, 1:2], epsc[:, 0:1], ALU.add)\
                    .then_inc(sem("isqF"), 1)
                pool.wait_ge(sem("isqF"), i.n + 1)
                pool.tensor_tensor(rstd[:, s:s + 1], small[:, s:s + 1], mhalf[:, 0:1], ALU.pow)\
                    .then_inc(sem("rstdF"), 1)
            run_steps(pool, T, 0, 2, norm_f)

        @block.scalar
        def _(act):
            act.wait_ge(sem("small_in"), 16 * 12)
            act.activation(tg[:, :], gates[:, :], ACT.Tanh).then_inc(sem("tg"), 1)
            act.activation(wdec[:, :], tdtf[:, 0, :], ACT.Exp).then_inc(sem("wdec"), 1)
            act.wait_ge(sem("wdec"), 1)
            act.activation(decay[:, :], wdec[:, :], ACT.Exp, scale=-1.0).then_inc(sem("decay"), 1)
            for n in range(8):
                act.wait_ge(sem("wT_ps"), n + 1)
                act.copy(attn_w[:, n // 2, n % 2, :], bank[6 + n % 2][:, 0:D]).then_inc(sem("wT"), 1)
            act.wait_ge(sem("negm"), 1)

            def wkv_exps(at):
                i = at(0)
                if i is None:
                    return
                n, s = i.n, i.slot
                act.wait_ge(sem("kvT"), n + 1)
                reach(act, sem("numden"), n - 1)
                reach(act, sem("yA"), n - 1)
                for c in range(C):
                    act.activation(ekm[s][:, c, :], bank[s][:, c * P:(c + 1) * P], ACT.Exp, bias=negm[:, c:c + 1])
                    ins = act.activation(eku[s][:, c, :], bank[s][:, c * P:(c + 1) * P], ACT.Exp,
                                         bias=umm[:, c:c + 1])
                ins.then_inc(sem("exps"), 1)
                act.copy(vTs[s], bank[2 + s][:, 0:D].rearrange("p (c n) -> p c n", c=C)).then_inc(sem("vTs"), 1)
            run_steps(act, T, 0, 2, wkv_exps)

            def route_act(at):
                i = at(0)
                if i is not None:
                    act.wait_ge(sem("h1T_ps"), i.n + 1)
                    reach(act, sem("h1T_all"), i.n - 1)
                    reach(act, sem("logits"), i.n - 1)
                    act.copy(h1Ts[i.slot], bank[i.slot][:, 0:D].rearrange("p (c n) -> p c n", c=C))\
                        .then_inc(sem("h1T"), 1)
                i = at(1)
                if i is not None:
                    act.wait_ge(sem("biased"), i.n + 1)
                    reach(act, sem("ck"), i.n - 1)
                    act.activation(pexp[i.slot], bank[2 + i.slot][:, 0:E], ACT.Exp, bias=nmx[i.slot])\
                        .then_inc(sem("pexp"), 1)
            run_steps(act, T, 1, 2, route_act)
            for n in range(8):
                act.wait_ge(sem("sup_ps"), n + 1)
                reach(act, sem("hs"), n - 1)
                act.activation(sgt[n % 2], bank[n % 2][:, :], ACT.Silu)
                act.copy(upt[n % 2], bank[2 + n % 2][:, :]).then_inc(sem("sgt"), 1)

            def moe_act(at):
                i = at(0, 2)
                if i is not None:
                    act.wait_ge(sem("xgT_ps"), i.n + 1)
                    reach(act, sem("gu"), i.n - 1)
                    act.copy(xgT[i.slot], bank[i.slot][:, 0:D].rearrange("p (c n) -> p c n", c=C))\
                        .then_inc(sem("xgT"), 1)
                i = at(1, 2)
                if i is not None:
                    act.wait_ge(sem("gu"), i.n + 1)
                    reach(act, sem("hb"), i.n - 1)
                    act.activation(sgb[i.slot], bank[2 + i.slot][:, 0:F], ACT.Silu).then_inc(sem("sgb"), 1)
            run_steps(act, NB, 1, 4, moe_act)

            def attn_act(at):
                i = at(0)
                if i is not None:
                    n, s = i.n, i.slot
                    act.wait_ge(sem("cTE_ps"), n + 1)
                    reach(act, sem("kv_ps"), n - 1)
                    act.copy(cTE[s], bank[5][:, 0:D].rearrange("p (c n) -> p c n", c=C)).then_inc(sem("cTE"), 1)
                    act.wait_ge(sem("xTE_ps"), n + 1)
                    reach(act, sem("q_ps"), n - 1)
                    act.copy(xTE[s], bank[5][:, 0:D].rearrange("p (c n) -> p c n", c=C)).then_inc(sem("xTE"), 1)
                    act.wait_ge(sem("kb"), n + 1)
                    act.activation(sq[1], kb[s], ACT.Square, accum_out=ssq[s][:, 1:2]).then_inc(sem("sq"), 1)
                    act.wait_ge(sem("qb"), n + 1)
                    act.activation(sq[0], qb[s], ACT.Square, accum_out=ssq[s][:, 0:1]).then_inc(sem("ssq"), 1)
                    act.wait_ge(sem("qT_ps"), n + 1)
                    reach(act, sem("S"), n - 1)
                    act.copy(qT[s], bank[5][:, :].rearrange("p (g n) -> p g n", g=4)).then_inc(sem("qT"), 1)
                    act.wait_ge(sem("kT_ps"), n + 1)
                    act.copy(kT[s], bank[4][:, :].rearrange("p (g n) -> p g n", g=4)).then_inc(sem("kT"), 1)
                    for j in range(4):
                        act.wait_ge(sem("shift"), 4 * n + j + 1)
                        act.activation(sS[:, j, :, :], sS[:, j, :, :], ACT.Exp).then_inc(sem("probs"), 1)
                    for j in range(4):
                        act.wait_ge(sem("pT_ps"), 4 * n + j + 1)
                        if j == 0:
                            reach(act, sem("pv"), n)
                        act.copy(pT[:, j, :, :], bank[6 + j % 2][:, :].rearrange("p (g n) -> p g n", g=4))\
                            .then_inc(sem("pT"), 1)
                    act.wait_ge(sem("oT_ps"), n + 1)
                    reach(act, sem("o_ps"), n - 1)
                    act.copy(oT[s], bank[5][:, 0:D].rearrange("p (c n) -> p c n", c=C)).then_inc(sem("oT"), 1)
            run_steps(act, T, 0, 2, attn_act)
            for n in range(12):
                act.wait_ge(sem("mxT_ps"), n + 1)
                src = bank[n % 2][:, :]
                if n < 8:
                    dst = mx_gu[:, :, n * 256:(n + 1) * 256].rearrange("p c (r o) -> p r c o", r=2)
                    act.copy(dst, src.rearrange("p (r c o) -> p r c o", r=2, c=C)).then_inc(sem("mxT"), 1)
                else:
                    r, q4 = (n - 8) // 2, (n - 8) % 2
                    dst = mx_dn[:, 4 * q4:4 * q4 + 4, r * P:(r + 1) * P]
                    act.copy(dst, src.rearrange("p (i o) -> p i o", i=4)).then_inc(sem("mxT"), 1)

            def ffn_act(at):
                i = at(0)
                n, s = i.n, i.slot
                act.wait_ge(sem("xTF_ps"), n + 1)
                reach(act, sem("gu8"), 4 * n - 4)
                act.copy(xTF[s], bank[0][:, 0:D].rearrange("p (c n) -> p c n", c=C)).then_inc(sem("xTF"), 1)
                for h in range(2):
                    act.wait_ge(sem("gu8"), 4 * n + h + 1)
                    reach(act, sem("hF"), 2 * n)
                    act.activation(sgF[:, h * 512:(h + 1) * 512], bank[2 + h][:, :], ACT.Silu)\
                        .then_inc(sem("sgF"), 1)
                for h in range(2):
                    act.wait_ge(sem("hTF_ps"), 2 * n + h + 1)
                    reach(act, sem("dF"), n - 1)
                    act.copy(hTF[s][:, 4 * h:4 * h + 4, :], bank[6 + h][:, :].rearrange("p (i n) -> p i n", i=4))\
                        .then_inc(sem("hTF"), 1)
            run_steps(act, T, 0, 2, ffn_act)

        @block.vector
        def _(dve):
            count = {}

            def chain(ins, name):
                ins.then_inc(sem(name), 1)
                count[name] = count.get(name, 0) + 1
                dve.wait_ge(sem(name), count[name])

            dve.wait_ge(sem("small_in"), 16 * 12)
            chain(dve.tensor_scalar(negm[:, :], tdtf[:, 1, :], 0.0, -1.0, ALU.max, ALU.mult), "r")
            dve.tensor_tensor(umm[:, :], tdtf[:, 1, :], negm[:, :], ALU.add).then_inc(sem("negm"), 1)
            dve.wait_ge(sem("x_in"), 16)
            for t in range(T):
                ins = dve.bn_stats(stats[:, t, :], x_res[:, t, :])
            ins.then_inc(sem("st"), 1)
            dve.wait_ge(sem("st"), 1)
            for t in range(T):
                dve.bn_aggr(mv[:, t, :], stats[:, t, :]).then_inc(sem("mv"), 1)
            dve.wait_ge(sem("rstd"), 1)
            dve.wait_ge(sem("decay"), 1)
            dve.wait_ge(sem("tg"), 1)
            dve.wait_ge(sem("const"), 14)

            def wkv(at):
                i = at(0)
                if i is not None:
                    reach(dve, sem("kvT"), i.n - 1)
                    dve.tensor_scalar(xnA[i.slot], x_res[:, i.n, :], mv[:, i.n, 0:1], rstd[:, bass.ds(i.n, 1)],
                                      ALU.subtract, ALU.mult).then_inc(sem("xnA"), 1)
                i = at(1)
                if i is not None:
                    n, s = i.n, i.slot
                    dve.wait_ge(sem("exps"), n + 1)
                    dve.wait_ge(sem("vTs"), n + 1)
                    reach(dve, sem("scan"), n - 1)
                    reach(dve, sem("numden"), n - 1)
                    dve.tensor_tensor(pm[s], ekm[s], vTs[s], ALU.mult).then_inc(sem("pm"), 1)
                    dve.wait_ge(sem("pm"), n + 1)
                    for c in range(C):
                        d = decay[:, c:c + 1].to_broadcast([P, P])
                        dve.tensor_tensor_scan(sB[s][:, c, 1:P + 1], d, ekm[s][:, c, :], 0.0, ALU.mult, ALU.add)
                        ins = dve.tensor_tensor_scan(sA[s][:, c, 1:P + 1], d, pm[s][:, c, :], 0.0,
                                                     ALU.mult, ALU.add)
                    ins.then_inc(sem("scan"), 1)
                i = at(2)
                if i is not None:
                    n, s = i.n, i.slot
                    dve.wait_ge(sem("numden"), n + 1)
                    reach(dve, sem("yT_ps"), n - 1)
                    dve.reciprocal(den[s], den[s]).then_inc(sem("rden"), 1)
                    dve.wait_ge(sem("rden"), n + 1)
                    dve.tensor_tensor(yA[s], num[s], den[s], ALU.mult).then_inc(sem("ym"), 1)
                    dve.wait_ge(sem("ym"), n + 1)
                    dve.tensor_copy(yA[s][:, :, 0:1], vTs[s][:, :, 0:1]).then_inc(sem("yA"), 1)
                i = at(3)
                if i is not None:
                    dve.wait_ge(sem("yT_ps"), i.n + 1)
                    dve.scalar_tensor_tensor(x_res[:, i.n, :], bank[4 + i.slot][:, 0:D], tg[:, GX0:GX0 + 1],
                                             x_res[:, i.n, :], ALU.mult, ALU.add).then_inc(sem("x1"), 1)
            run_steps(dve, T, 3, 2, wkv, lead=2)

            def route(at):
                i = at(0)
                if i is not None:
                    n, s = i.n, i.slot
                    wait_apart(dve, (sem("const"), 14), (sem("x1"), n + 1), (sem("h1"), n - 1))
                    dve.bn_stats(stats[:, s, :], x_res[:, n, :]).then_inc(sem("stB"), 1)
                    wait_apart(dve, (sem("const"), 14), (sem("stB"), n + 1))
                    dve.bn_aggr(mv[:, s, :], stats[:, s, :]).then_inc(sem("mvB"), 1)
                i = at(1)
                if i is not None:
                    n, s = i.n, i.slot
                    dve.wait_ge(sem("rstdB"), n + 1)
                    dve.wait_ge(sem("mvB"), n + 1)
                    if not (isinstance(n, int) and n < 2):
                        dve.wait_ge(sem(f"h1_out{s}"), 16 * i.lap)
                        dve.wait_ge(sem("h1T_ps"), n - 1)
                    dve.tensor_scalar(h1B[s], x_res[:, n, :], mv[:, s, 0:1], rstd[:, s:s + 1],
                                      ALU.subtract, ALU.mult).then_inc(sem("h1"), 1)
                i = at(2)
                if i is not None:
                    n, s = i.n, i.slot
                    wait_apart(dve, (sem("const"), 14), (sem("logits"), n + 1), (sem("rc"), n - 1))
                    dve.tensor_reduce(nmx[s], bank[2 + s][:, 0:E], AX.X, ALU.max, negate=True)
                    dve.tensor_tensor(biased[s], bank[2 + s][:, 0:E], rbias[:, :], ALU.add).then_inc(sem("biased"), 1)
                    wait_apart(dve, (sem("const"), 14), (sem("biased"), n + 1))
                    dve.max(v8, biased[s]).then_inc(sem("pick"), 1)
                    wait_apart(dve, (sem("const"), 14), (sem("pick"), 4 * n + 1))
                    dve.max_index(i8, v8, biased[s]).then_inc(sem("pick"), 1)
                    dve.wait_ge(sem("pick"), 4 * n + 2)
                    dve.tensor_copy(i8f, i8).then_inc(sem("pick"), 1)
                    dve.wait_ge(sem("pick"), 4 * n + 3)
                    dve.tensor_tensor(onehot[:, n, :, :], iota[:, 0:E].unsqueeze(1).to_broadcast([P, K, E]),
                                      i8f[:, 0:K].unsqueeze(2).to_broadcast([P, K, E]), ALU.is_equal)\
                        .then_inc(sem("pick"), 1)
                    wait_apart(dve, (sem("const"), 14), (sem("pick"), 4 * n + 4), (sem("macc"), n - 1), (sem("rank"), n - 1))
                    with nc.allow_low_precision("counts of at most 8 are exact in bfloat16"):
                        dve.tensor_reduce(mask[s], onehot[:, n, :, :].rearrange("p k e -> p e k"), AX.X, ALU.add)\
                            .then_inc(sem("mask"), 1)
                i = at(3)
                if i is not None:
                    n, s = i.n, i.slot
                    dve.wait_ge(sem("pexp"), n + 1)
                    dve.tensor_tensor(prod, onehot[:, n, :, :], pexp[s].unsqueeze(1).to_broadcast([P, K, E]), ALU.mult)
                    dve.wait_ge(sem("rank"), n + 1)
                    dve.tensor_tensor(prod2, onehot[:, n, :, :],
                                      bank[4 + s][:, 0:E].unsqueeze(1).to_broadcast([P, K, E]), ALU.mult)\
                        .then_inc(sem("prod"), 1)
                    wait_apart(dve, (sem("const"), 14), (sem("prod"), n + 1))
                    dve.tensor_reduce(ck, prod, AX.X, ALU.add).then_inc(sem("ck"), 1)
                    dve.tensor_reduce(rank_all[:, n, :], prod2, AX.X, ALU.add)
                    wait_apart(dve, (sem("const"), 14), (sem("ck"), n + 1))
                    dve.tensor_reduce(cs, ck, AX.X, ALU.add).then_inc(sem("share"), 1)
                    dve.wait_ge(sem("share"), 2 * n + 1)
                    dve.reciprocal(rcs, cs).then_inc(sem("share"), 1)
                    dve.wait_ge(sem("share"), 2 * n + 2)
                    dve.tensor_scalar(combs[:, n, :], ck, rcs[:, 0:1], tg[:, GF0:GF0 + 1], ALU.mult, ALU.mult)\
                        .then_inc(sem("rc"), 1)
            run_steps(dve, T, 3, 2, route, lead=2)

            dve.wait_ge(sem("counts"), 1)
            chain(dve.tensor_scalar(cnt_i, bank[6][:, 0:E], float(P - 1), None, ALU.add), "r")
            chain(dve.tensor_scalar(nb_i, cnt_i, 7, None, ALU.logical_shift_right), "r")
            chain(dve.tensor_copy(nbf, nb_i), "r")
            chain(dve.tensor_tensor_scan(cum, ones[:, 0:E], nbf, 0.0, ALU.mult, ALU.add), "r")
            dve.tensor_scalar(cmp, cum, pcol[:, 0:1], None, ALU.is_le)
            chain(dve.tensor_tensor(base, cum, nbf, ALU.subtract), "r")
            chain(dve.tensor_reduce(eidf, cmp, AX.X, ALU.add), "r")
            dve.tensor_scalar(eidm, eidf, float(E - 1), None, ALU.min).then_inc(sem("eidm"), 1)
            chain(dve.tensor_scalar(base, base, float(P), None, ALU.mult), "r")
            chain(dve.tensor_tensor(tmp, onehot.rearrange("p t k e -> p (t k) e"),
                                    base.unsqueeze(1).to_broadcast([P, T * K, E]), ALU.mult), "r")
            chain(dve.tensor_reduce(sbase, tmp, AX.X, ALU.add), "r")
            chain(dve.tensor_tensor(slotf, sbase, rank_all[:, :, :].rearrange("p t k -> p (t k)"), ALU.add), "r")
            dve.tensor_copy(slot_u[:, :], slotf).then_inc(sem("slot_u"), 1)
            chain(dve.tensor_copy(slot_i, slotf), "r")
            dve.tensor_scalar(blk_i, slot_i, 7, None, ALU.logical_shift_right)
            chain(dve.tensor_scalar(pos_i, slot_i, P - 1, None, ALU.bitwise_and), "r")
            dve.tensor_copy(blkf, blk_i)
            chain(dve.tensor_copy(posf, pos_i), "r")
            dve.wait_ge(sem("eid_ps"), 1)
            dve.tensor_copy(eid_row[:, :], bank[7][0:1, 0:P]).then_inc(sem("eid"), 1)

            def table(at):
                i = at(0)
                if i is None:
                    return
                n, s = i.n, i.slot
                reach(dve, sem("tab_ps"), n - 3)
                dve.tensor_scalar(poh[s], iota[:, :], posf[:, bass.ds(n, 1)], None, ALU.is_equal)
                dve.tensor_scalar(boh[s], iota[:, 0:NB], blkf[:, bass.ds(n, 1)], tokid[:, bass.ds(i.lap, 1)],
                                  ALU.is_equal, ALU.mult).then_inc(sem("onehots"), 1)
            run_steps(dve, T * K, 0, 4, table)
            dve.wait_ge(sem("tab_ps"), T * K)
            dve.tensor_copy(tokf[:, :], bank[5][:, 0:NB]).then_inc(sem("tok"), 1)

            for t in range(T):
                dve.wait_ge(sem("sdown"), t + 1)
                dve.scalar_tensor_tensor(x_res[:, t, :], bank[2 + t % 2][:, 0:D], tg[:, GF0:GF0 + 1],
                                         x_res[:, t, :], ALU.mult, ALU.add).then_inc(sem("xs"), 1)

            def moe_dve(at):
                i = at(0, 2)
                if i is not None:
                    dve.wait_ge(sem("sgb"), i.n + 1)
                    reach(dve, sem("hT_ps"), i.n - 1)
                    dve.tensor_tensor(hb[i.slot], bank[2 + i.slot][:, F:2 * F], sgb[i.slot], ALU.mult)\
                        .then_inc(sem("hb"), 1)
                i = at(1, 2)
                if i is not None:
                    dve.wait_ge(sem("hT_ps"), i.n + 1)
                    reach(dve, sem("mo_y"), i.n - 1)
                    dve.tensor_copy(hbT[i.slot][0:F, :], bank[4 + i.slot][0:F, 0:P]).then_inc(sem("hbT"), 1)
                i = at(2, 2)
                if i is not None:
                    dve.wait_ge(sem("mo_y"), i.n + 1)
                    if not (isinstance(i.n, int) and i.n < 2):
                        dve.wait_ge(sem(f"ys_out{i.slot}"), 16 * i.lap)
                    dve.tensor_copy(ysb[i.slot], bank[6 + i.slot][:, 0:D]).then_inc(sem("ysb"), 1)
            run_steps(dve, NB, 2, 4, moe_dve)

            dve.wait_ge(sem("gu"), NB)
            dve.wait_ge(sem("padE"), 6)
            dve.tensor_scalar(bias_bc[:, NQ_, :], bias_bc[:, NQ_, :], (D / HD) ** 0.5, None, ALU.mult)\
                .then_inc(sem("gob"), 1)
            dve.tensor_scalar(bias_bc[:, NK_, :], bias_bc[:, NK_, :], D ** 0.5, None, ALU.mult)\
                .then_inc(sem("gob"), 1)
            dve.tensor_scalar(gob, bias_bc[:, OB_, :], tg[:, GX1:GX1 + 1], None, ALU.mult).then_inc(sem("gob"), 1)
            dve.wait_ge(sem("gob"), 3)
            dve.wait_ge(sem("xs"), T)

            def attn_head(i):
                n, s = i.n, i.slot
                dve.wait_ge(sem(f"yk{s}"), 64 * (i.lap + 1))
                for k in range(K):
                    dve.scalar_tensor_tensor(x_res[:, n, :], yk[s][k], combs[:, n, k:k + 1], x_res[:, n, :],
                                             ALU.mult, ALU.add).then_inc(sem("x2k"), 1)
                    wait_apart(dve, (sem("const"), 14), (sem("x2k"), n * K + k + 1))
                dve.bn_stats(stats[:, s, :], x_res[:, n, :]).then_inc(sem("x2"), 1)
                wait_apart(dve, (sem("const"), 14), (sem("x2"), n + 1))
                dve.bn_aggr(mv[:, s, :], stats[:, s, :]).then_inc(sem("mvE"), 1)

            def attn(at):
                i = at(0)
                if i is not None:
                    attn_head(i)
                i = at(0)
                if i is None:
                    return
                n, s = i.n, i.slot
                dve.wait_ge(sem("kv_ps"), n + 1)
                reach(dve, sem("ssq"), n - 1)
                dve.tensor_tensor(kb[s], bank[4][:, 0:D], bias_bc[:, KB_, :], ALU.add).then_inc(sem("kb"), 1)
                reach(dve, sem("pv"), n - 1)
                dve.tensor_tensor(va[s][:, :, 0:HD], bank[4][:, D:2 * D].rearrange("p (h d) -> p h d", h=H),
                                  bias_bc[:, VB_, :].rearrange("p (h d) -> p h d", h=H), ALU.add)\
                    .then_inc(sem("va"), 1)
                dve.wait_ge(sem("rstdE"), n + 1)
                dve.wait_ge(sem("mvE"), n + 1)
                reach(dve, sem("xTE_ps"), n - 1)
                dve.tensor_scalar(xnE[s], x_res[:, n, :], mv[:, s, 0:1], rstd[:, s:s + 1],
                                  ALU.subtract, ALU.mult).then_inc(sem("xnE"), 1)
                dve.wait_ge(sem("q_ps"), n + 1)
                dve.tensor_tensor(qb[s], bank[5][:, 0:D], bias_bc[:, QB_, :], ALU.add).then_inc(sem("qb"), 1)
                dve.wait_ge(sem("rq"), n + 1)
                dve.wait_ge(sem("qb"), n + 1)
                reach(dve, sem("kT_ps"), n - 1)
                for raw, col, norm, dst, name in ((qb, 0, NQ_, qn, "qn"), (kb, 1, NK_, kn, "kn")):
                    dve.scalar_tensor_tensor(dst[s][:, :, 0:HD], raw[s].rearrange("p (h d) -> p h d", h=H),
                                             rq[s][:, col:col + 1],
                                             bias_bc[:, norm, :].rearrange("p (h d) -> p h d", h=H),
                                             ALU.mult, ALU.mult).then_inc(sem(name), 1)
                reach(dve, sem("pT_ps"), 4 * n)
                for j in range(4):
                    dve.wait_ge(sem("S"), n + 1)
                    src = bank[j][:, :].rearrange("p (g k) -> p g k", g=4)
                    dve.tensor_reduce(smax[s][:, 4 * j:4 * j + 4], src, AX.X, ALU.max).then_inc(sem("smax"), 1)
                    dve.wait_ge(sem("smax"), 4 * n + j + 1)
                    dve.tensor_tensor(sS[:, j, :, :], src,
                                      smax[s][:, 4 * j:4 * j + 4].unsqueeze(2).to_broadcast([P, 4, P]),
                                      ALU.subtract).then_inc(sem("shift"), 1)
                dve.wait_ge(sem("pv"), n + 1)
                pv = bank[4][:, 0:H * (HD + 1)].rearrange("p (h d) -> p h d", h=H)
                dve.reciprocal(rsum[s], pv[:, :, HD:HD + 1].rearrange("p h a -> p (h a)")).then_inc(sem("rsum"), 1)
                dve.wait_ge(sem("rsum"), n + 1)
                reach(dve, sem("oT_ps"), n - 1)
                dve.tensor_tensor(oE[s], pv[:, :, 0:HD], rsum[s].unsqueeze(2).to_broadcast([P, H, HD]), ALU.mult)\
                    .then_inc(sem("oE"), 1)
                dve.tensor_tensor(x_res[:, n, :], x_res[:, n, :], gob, ALU.add).then_inc(sem("x3a"), 1)
                dve.wait_ge(sem("o_ps"), n + 1)
                dve.wait_ge(sem("x3a"), n + 1)
                dve.scalar_tensor_tensor(x_res[:, n, :], bank[5][:, 0:D], tg[:, GX1:GX1 + 1], x_res[:, n, :],
                                         ALU.mult, ALU.add).then_inc(sem("x3"), 1)
            run_steps(dve, T, 0, 2, attn)

            def quantise(src, width, mx, sc, rs, y, e, a, dst, before, done):
                nblk = width // QB
                b3 = "p (b w) -> p b w"

                def wide(v):
                    return v.unsqueeze(2).to_broadcast([P, nblk, QB])

                def link(ins, k):
                    ins.then_inc(sem("quant"), 1)
                    dve.wait_ge(sem("quant"), before + k)
                link(dve.tensor_reduce(mx, src.rearrange(b3, w=QB), AX.X, ALU.max, apply_absolute_value=True), 1)
                link(dve.tensor_scalar(sc, mx, 1.0 / FP8_MAX, 1e-30, ALU.mult, ALU.max), 2)
                link(dve.reciprocal(rs, sc), 3)
                link(dve.tensor_tensor(y.rearrange(b3, w=QB), src.rearrange(b3, w=QB), wide(rs), ALU.mult), 4)
                link(dve.tensor_scalar(e.bitcast(U32), y.bitcast(U32), EXPONENT, None, ALU.bitwise_and), 5)
                link(dve.tensor_scalar(e, e, FP8_TINY, ROUND4, ALU.max, ALU.mult), 6)
                link(dve.tensor_tensor(a, y, e, ALU.add), 7)
                link(dve.tensor_tensor(a, a, e, ALU.subtract), 8)
                dve.tensor_tensor(dst.rearrange(b3, w=QB), a.rearrange(b3, w=QB), wide(sc), ALU.mult)\
                    .then_inc(sem(done), 1)

            for n in range(6):
                dve.wait_ge(sem(f"wn_in{n % 2}"), 16 * (n // 2 + 1))
                reach(dve, sem("mxT_ps"), 2 * n - 2)
                reach(dve, sem("w_deq"), n)
                quantise(wn[n % 2], 1024, wam, wac, war, wq[n % 2], we, wa, wq[n % 2], 8 * n, "w_deq")
            dve.wait_ge(sem("x3"), T)

            def ffn(at):
                i = at(0)
                n, s = i.n, i.slot
                dve.wait_ge(sem("x3"), T)
                dve.bn_stats(stats[:, s, :], x_res[:, n, :]).then_inc(sem("stF"), 1)
                wait_apart(dve, (sem("const"), 14), (sem("stF"), n + 1))
                dve.bn_aggr(mv[:, s, :], stats[:, s, :]).then_inc(sem("mvF"), 1)
                dve.wait_ge(sem("rstdF"), n + 1)
                dve.wait_ge(sem("mvF"), n + 1)
                dve.tensor_scalar(xnF[s], x_res[:, n, :], mv[:, s, 0:1], rstd[:, s:s + 1],
                                  ALU.subtract, ALU.mult).then_inc(sem("xnF"), 1)
                dve.wait_ge(sem("xnF"), n + 1)
                reach(dve, sem("xTF_ps"), n - 1)
                quantise(xnF[s], D, amx, amc, arc, xyF, xeF, xaF, xqF[s], 48 + 16 * n, "xqF")
                for h in range(2):
                    dve.wait_ge(sem("sgF"), 2 * n + h + 1)
                    dve.wait_ge(sem("gu8"), 4 * n + 2 + h + 1)
                    dve.tensor_tensor(hF[:, h * 512:(h + 1) * 512], bank[4 + h][:, :],
                                      sgF[:, h * 512:(h + 1) * 512], ALU.mult).then_inc(sem("hF"), 1)
                dve.wait_ge(sem("hF"), 2 * n + 2)
                reach(dve, sem("hTF_ps"), 2 * n - 2)
                quantise(hF, INNER, amh, ahc, ahr, sgF, heF, haF, hqF[s], 56 + 16 * n, "hqF")
                dve.wait_ge(sem("dF"), n + 1)
                dve.scalar_tensor_tensor(x_res[:, n, :], bank[1][:, 0:D], tg[:, GF1:GF1 + 1], x_res[:, n, :],
                                         ALU.mult, ALU.add).then_inc(sem("x4"), 1)
            run_steps(dve, T, 0, 2, ffn)

        @block.tensor
        def _(pe):
            pe.wait_ge(sem("const"), 14)

            def turn(dst, src, m=P, k=P):
                return pe.transpose(dst, src, ident[0:k, 0:k])

            pe.wait_ge(sem("wnat_in"), 64)
            for n in range(8):
                w, c = n // 2, n % 2
                reach(pe, sem("wT"), n - 1)
                for o in range(2):
                    ins = turn(bank[6 + n % 2][:, o * P:(o + 1) * P], w_nat[:, w, o, c * P:(c + 1) * P])
                ins.then_inc(sem("wT_ps"), 1)

            def wkv_pe(at):
                i = at(0)
                if i is not None:
                    n, s = i.n, i.slot
                    pe.wait_ge(sem("xnA"), n + 1)
                    pe.wait_ge(sem(f"cxA_in{s}"), 16 * (i.lap + 1))
                    reach(pe, sem("exps"), n - 1)
                    reach(pe, sem("vTs"), n - 1)
                    for c in range(C):
                        turn(bank[s][:, c * P:(c + 1) * P], xnA[s][:, c * P:(c + 1) * P])
                        ins = turn(bank[2 + s][:, c * P:(c + 1) * P], cxA[s][:, c * P:(c + 1) * P])
                    ins.then_inc(sem("kvT"), 1)
                i = at(2)
                if i is not None:
                    n, s = i.n, i.slot
                    pe.wait_ge(sem("yA"), n + 1)
                    reach(pe, sem("x1"), n - 1)
                    for c in range(C):
                        ins = turn(bank[4 + s][:, c * P:(c + 1) * P], yA[s][:, c, :])
                    ins.then_inc(sem("yT_ps"), 1)
            run_steps(pe, T, 2, 2, wkv_pe, lead=2)

            def route_pe(at):
                i = at(0)
                if i is not None:
                    n, s = i.n, i.slot
                    pe.wait_ge(sem("h1"), n + 1)
                    reach(pe, sem("h1T"), n - 1)
                    for c in range(C):
                        ins = turn(bank[s][:, c * P:(c + 1) * P], h1B[s][:, c * P:(c + 1) * P])
                    ins.then_inc(sem("h1T_ps"), 1)
                    pe.wait_ge(sem("h1T"), n + 1)
                    reach(pe, sem("pexp"), n - 1)
                    reach(pe, sem("biased"), n - 1)
                    for c in range(C):
                        ins = pe.matmul(bank[2 + s][:, 0:E], h1Ts[s][:, c, :], router_sb[:, c, :],
                                        start=(c == 0), stop=(c == C - 1))
                    ins.then_inc(sem("logits"), 1)
                i = at(1)
                if i is not None:
                    n, s = i.n, i.slot
                    pe.wait_ge(sem("mask"), n + 1)
                    reach(pe, sem("macc"), n)
                    reach(pe, sem("ck"), n - 1)
                    pe.matmul(bank[4 + s][:, 0:E], tri[:, :], mask[s], start=True, stop=False)
                    pe.matmul(bank[4 + s][:, 0:E], ones[:, :], macc[:, s, :], start=False, stop=True)\
                        .then_inc(sem("rank"), 1)
            run_steps(pe, T, 1, 2, route_pe)
            pe.wait_ge(sem("macc"), T)
            pe.matmul(bank[6][:, 0:E], ones[:, :], macc[:, 0, :], start=True, stop=True).then_inc(sem("counts"), 1)

            pe.wait_ge(sem("shared_in"), 6 * 16)
            pe.wait_ge(sem("pexp"), T)
            pe.wait_ge(sem("h1T_all"), T)
            for n in range(8):
                f, hf = n % 4, n // 4
                reach(pe, sem("sgt"), n - 1)
                for part in range(2):
                    for c in range(C):
                        ins = pe.matmul(bank[2 * part + n % 2][:, :], sgu_w[:, c, part * SH + f * P:part * SH + (f + 1) * P],
                                        h1T[:, c, hf * 512:(hf + 1) * 512], start=(c == 0), stop=(c == C - 1))
                ins.then_inc(sem("sup_ps"), 1)
                if n == 3:
                    pe.wait_ge(sem("eidm"), 1)
                    pe.matmul(bank[7][0:1, 0:P], eidm, ident[:, :], start=True, stop=True).then_inc(sem("eid_ps"), 1)
            pe.wait_ge(sem("rc"), T)

            def table_pe(at):
                i = at(0)
                if i is None:
                    return
                pe.wait_ge(sem("onehots"), i.n + 1)
                first = isinstance(i.n, int) and i.n == 0
                last = isinstance(i.n, int) and i.n == T * K - 1
                pe.matmul(bank[5][:, 0:NB], poh[i.slot], boh[i.slot], start=first, stop=last)\
                    .then_inc(sem("tab_ps"), 1)
            run_steps(pe, T * K, 0, 4, table_pe, tail=4)
            pe.wait_ge(sem("sgt"), 8)
            pe.wait_ge(sem("hs"), 8)
            for t in range(T):
                reach(pe, sem("xs"), t - 1)
                for f in range(4):
                    ins = pe.matmul(bank[2 + t % 2][:, 0:D], hs[:, f, t * P:(t + 1) * P], sd_w[:, f, :],
                                    start=(f == 0), stop=(f == 3))
                ins.then_inc(sem("sdown"), 1)

            pe.wait_ge(sem("moe_in"), 16 * 18)
            pe.wait_ge(sem("moe_in2"), 16 * 2)
            pe.wait_ge(sem("eid"), 1)
            pe.wait_ge(sem("tok"), 1)
            pe.wait_ge(sem("xs"), T)

            def expert_of(n):
                return pe.value_load(eid_row[0:1, bass.ds(n, 1)], min_val=0, max_val=E - 1)

            def moe_pe(at):
                i, i2 = at(0), at(0, 2)
                if i is not None:
                    pe.wait_ge(sem(f"xg{i.slot}"), 16 * (i.lap + 1))
                    reach(pe, sem("xgT"), i.n - 1)
                    for c in range(C):
                        ins = turn(bank[i2.slot][:, c * P:(c + 1) * P], xg[i.slot][:, c * P:(c + 1) * P])
                    ins.then_inc(sem("xgT_ps"), 1)
                i = at(1, 2)
                if i is not None:
                    e = expert_of(i.n)
                    pe.wait_ge(sem("xgT"), i.n + 1)
                    reach(pe, sem("hb"), i.n - 1)
                    for c in range(C):
                        ins = pe.matmul(bank[2 + i.slot][:, 0:2 * F], xgT[i.slot][:, c, :],
                                        moe_up[:, c, bass.ds(e, 1), :].rearrange("p a f -> p (a f)"),
                                        start=(c == 0), stop=(c == C - 1))
                    ins.then_inc(sem("gu"), 1)
                i = at(2, 2)
                if i is not None:
                    wait_apart(pe, (sem("tok"), 1), (sem("hb"), i.n + 1), (sem("hbT"), i.n - 1))
                    turn(bank[4 + i.slot][0:F, 0:P], hb[i.slot]).then_inc(sem("hT_ps"), 1)
                i = at(3, 2)
                if i is not None:
                    e = expert_of(i.n)
                    pe.wait_ge(sem("hbT"), i.n + 1)
                    reach(pe, sem("ysb"), i.n - 1)
                    pe.matmul(bank[6 + i.slot][:, 0:D], hbT[i.slot][0:F, :],
                              moe_dn[:, bass.ds(e, 1), :].rearrange("p a d -> p (a d)"),
                              start=True, stop=True).then_inc(sem("mo_y"), 1)
            run_steps(pe, NB, 3, 4, moe_pe)
            pe.wait_ge(sem("ysb"), NB)

            def attn_pe(at):
                i = at(0)
                n, s = i.n, i.slot
                pe.wait_ge(sem(f"cxE_in{s}"), 16 * (i.lap + 1))
                reach(pe, sem("x3"), n)
                for c in range(C):
                    ins = turn(bank[5][:, c * P:(c + 1) * P], cxE[s][:, c * P:(c + 1) * P])
                ins.then_inc(sem("cTE_ps"), 1)
                pe.wait_ge(sem("cTE"), n + 1)
                reach(pe, sem("oE"), n)
                for w in (1, 2):
                    for c in range(C):
                        ins = pe.matmul(bank[4][:, (w - 1) * D:w * D], cTE[s][:, c, :], attn_w[:, w, c, :],
                                        start=(c == 0), stop=(c == C - 1))
                ins.then_inc(sem("kv_ps"), 1)
                pe.wait_ge(sem("xnE"), n + 1)
                for c in range(C):
                    ins = turn(bank[5][:, c * P:(c + 1) * P], xnE[s][:, c * P:(c + 1) * P])
                ins.then_inc(sem("xTE_ps"), 1)
                pe.wait_ge(sem("xTE"), n + 1)
                for c in range(C):
                    ins = pe.matmul(bank[5][:, 0:D], xTE[s][:, c, :], attn_w[:, 0, c, :],
                                    start=(c == 0), stop=(c == C - 1))
                ins.then_inc(sem("q_ps"), 1)
                pe.wait_ge(sem("qn"), n + 1)
                for g in range(4):
                    ins = turn(bank[5][:, g * P:(g + 1) * P],
                               qn[s][:, 4 * g:4 * g + 4, :].rearrange("p h d -> p (h d)"))
                ins.then_inc(sem("qT_ps"), 1)
                pe.wait_ge(sem("kn"), n + 1)
                pe.wait_ge(sem("va"), n + 1)
                for g in range(4):
                    ins = turn(bank[4][:, g * P:(g + 1) * P],
                               kn[s][:, 4 * g:4 * g + 4, :].rearrange("p h d -> p (h d)"))
                ins.then_inc(sem("kT_ps"), 1)
                pe.wait_ge(sem("qT"), n + 1)
                pe.wait_ge(sem("kT"), n + 1)
                reach(pe, sem("shift"), 4 * n)
                for g in range(4):
                    for j in range(4):
                        rows = slice(HP * j, HP * j + HP)
                        ins = pe.matmul(bank[j][:, g * P:(g + 1) * P], qT[s][rows, g, :], kT[s][rows, g, :],
                                        start=True, stop=True)
                ins.then_inc(sem("S"), 1)
                for j in range(4):
                    pe.wait_ge(sem("probs"), 4 * n + j + 1)
                    reach(pe, sem("pT"), 4 * n + j - 1)
                    for g in range(4):
                        ins = turn(bank[6 + j % 2][:, g * P:(g + 1) * P], sS[:, j, g, :])
                    ins.then_inc(sem("pT_ps"), 1)
                for j in range(4):
                    pe.wait_ge(sem("pT"), 4 * n + j + 1)
                    for g in range(4):
                        h = 4 * g + j
                        ins = pe.matmul(bank[4][:, h * (HD + 1):(h + 1) * (HD + 1)], pT[:, j, g, :],
                                        va[s][:, h, :], start=True, stop=True)
                ins.then_inc(sem("pv"), 1)
                pe.wait_ge(sem("oE"), n + 1)
                for c in range(C):
                    ins = turn(bank[5][:, c * P:(c + 1) * P],
                               oE[s].rearrange("p h d -> p (h d)")[:, c * P:(c + 1) * P])
                ins.then_inc(sem("oT_ps"), 1)
                pe.wait_ge(sem("oT"), n + 1)
                for c in range(C):
                    ins = pe.matmul(bank[5][:, 0:D], oT[s][:, c, :], attn_w[:, 3, c, :],
                                    start=(c == 0), stop=(c == C - 1))
                ins.then_inc(sem("o_ps"), 1)
            run_steps(pe, T, 0, 2, attn_pe)
            pe.wait_ge(sem("shift"), 4 * T)
            for n in range(12):
                pe.wait_ge(sem("w_deq"), (n // 2) + 1)
                reach(pe, sem("mxT"), n - 1)
                for k in range(4):
                    ins = turn(bank[n % 2][:, k * P:(k + 1) * P],
                               wq[(n // 2) % 2][:, (n % 2) * 512 + k * P:(n % 2) * 512 + (k + 1) * P])
                ins.then_inc(sem("mxT_ps"), 1)
            pe.wait_ge(sem("mxT"), 12)
            pe.wait_ge(sem("x3"), T)

            def ffn_pe(at):
                i = at(0)
                n, s = i.n, i.slot
                pe.wait_ge(sem("xqF"), n + 1)
                for c in range(C):
                    ins = turn(bank[0][:, c * P:(c + 1) * P], xqF[s][:, c * P:(c + 1) * P])
                ins.then_inc(sem("xTF_ps"), 1)
                pe.wait_ge(sem("xTF"), n + 1)
                reach(pe, sem("hF"), 2 * n)
                for q in range(4):
                    for c in range(C):
                        ins = pe.matmul(bank[2 + q][:, :], xTF[s][:, c, :], mx_gu[:, c, q * 512:(q + 1) * 512],
                                        start=(c == 0), stop=(c == C - 1))
                    ins.then_inc(sem("gu8"), 1)
                pe.wait_ge(sem("hqF"), n + 1)
                reach(pe, sem("hTF"), 2 * n)
                for h in range(2):
                    for k in range(4):
                        ins = turn(bank[6 + h][:, k * P:(k + 1) * P], hqF[s][:, h * 512 + k * P:h * 512 + (k + 1) * P])
                    ins.then_inc(sem("hTF_ps"), 1)
                pe.wait_ge(sem("hTF"), 2 * n + 2)
                reach(pe, sem("x4"), n)
                for k in range(8):
                    ins = pe.matmul(bank[1][:, 0:D], hTF[s][:, k, :], mx_dn[:, k, :], start=(k == 0), stop=(k == 7))
                ins.then_inc(sem("dF"), 1)
            run_steps(pe, T, 0, 2, ffn_pe)


_INS = ['x', 'ctx_2048', 'g_xattn', 'g_ffn', 'L0_xattn_time_decay', 'L0_xattn_time_first',
        'L0_ffn_router_w', 'L0_ffn_router_bias', 'L0_ffn_wg', 'L0_ffn_wu', 'L0_ffn_wd', 'L0_ffn_swg',
        'L0_ffn_swu', 'L0_ffn_swd', 'L1_xattn_q_w', 'L1_xattn_q_b', 'L1_xattn_k_img_w',
        'L1_xattn_k_img_b', 'L1_xattn_v_img_w', 'L1_xattn_v_img_b', 'L1_xattn_o_w', 'L1_xattn_o_b',
        'L1_xattn_norm_q_w', 'L1_xattn_norm_k_img_w', 'L1_ffn_gate_w', 'L1_ffn_up_w', 'L1_ffn_down_w']


def kernel(**inputs):
    import numpy as _np
    import concourse.bacc as _bacc
    from concourse import mybir as _mybir
    from concourse.bass_utils import run_bass_kernel_spmd as _run

    nc = _bacc.Bacc("TRN2", target_bir_lowering=False, num_devices=1)
    arrays, args = {}, []
    for name in _INS:
        a = _np.ascontiguousarray(inputs[name])
        arrays[f"in_{name}_dram"] = a
        args.append(nc.dram_tensor(f"in_{name}_dram", a.shape, _mybir.dt.from_np(a.dtype), kind="ExternalInput").ap())
    out = nc.dram_tensor("out_dram", (T, P, D), F32, kind="ExternalOutput").ap()
    build_program(nc, *args, out)
    r = _run(nc, [arrays], core_ids=[0])
    return r.results[0]["out_dram"]
```

```python
from contextlib import ExitStack

import concourse.bass as bass
from concourse import mybir

ALU = mybir.AluOpType
ACT = mybir.ActivationFunctionType
AX = mybir.AxisListType
F32 = mybir.dt.float32
F16 = mybir.dt.float16
BF16 = mybir.dt.bfloat16
I32 = mybir.dt.int32
U32 = mybir.dt.uint32

P = 128
D = 256
C = D // P
T = 8
N = T * P
E = 64
F = 64
K = 4
NB = 96
SH = 512
H = 16
HD = D // H
HP = 32
INNER = 1024
QB = 32
LN_EPS = 1e-5
RMS_EPS = 1e-6
FP8_MAX = 448.0
FP8_TINY = 2.0 ** -6
ROUND4 = 1.5 * 2.0 ** 20
EXPONENT = 0x7F800000


class Item:

    def __init__(self, n, slot, lap):
        self.n, self.slot, self.lap = n, slot, lap


def run_steps(eng, items, depth, unroll, body, lead=1, tail=0):

    def step(g, k):
        def at(d=0, slots=unroll):
            lap, slot = (k - d) // unroll, (k - d) % unroll
            n = g * unroll + (k - d)
            if isinstance(g, int) and not 0 <= n < items:
                return None
            per = unroll // slots
            return Item(n, slot % slots, (g + lap) * per + slot // slots)
        body(at)

    whole = (items - tail) // unroll
    lead = min(lead, whole)
    for s in range(lead * unroll):
        step(s // unroll, s % unroll)
    if whole > lead:
        with eng.Fori(lead, whole) as g:
            for k in range(unroll):
                step(g, k)
    for s in range(whole * unroll, items + depth):
        step(s // unroll, s % unroll)


def reach(eng, sem, value):
    if isinstance(value, int) and value <= 0:
        return
    eng.wait_ge(sem, value)


def wait_apart(eng, met, *waits):
    waits = [(s, v if isinstance(v, int) else eng.to_reg(v)) for s, v in waits
             if not (isinstance(v, int) and v <= 0)]
    eng.wait_ge(*met)
    for s, v in waits:
        eng.wait_ge(s, v)


def build_program(nc, x, ctx_in, g_xattn, g_ffn, time_decay, time_first, router_w, router_bias,
                  wg, wu, wd, swg, swu, swd, q_w, q_b, k_w, k_b, v_w, v_b, o_w, o_b,
                  norm_q_w, norm_k_w, gate_w, up_w, down_w, out):
    h1_dram = nc.dram_tensor("h1_dram", (N, D), F32, kind="Internal").ap()
    ys_dram = nc.dram_tensor("ys_dram", (NB * P, D), F32, kind="Internal").ap()

    with ExitStack() as ctx:
        def sb(name, shape, dt=F32):
            return ctx.enter_context(nc.sbuf_tensor(name, shape, dt))

        sems = {}

        def sem(name):
            if name not in sems:
                sems[name] = ctx.enter_context(nc.semaphore(name))
            return sems[name]

        bank = [ctx.enter_context(nc.psum_tensor(f"bank{i}", [P, 512], F32)) for i in range(8)]

        arena_up = sb("arena_up", [P, C * E * 2 * F])
        arena_dn = sb("arena_dn", [P, E * D])
        moe_up = arena_up[:, :].rearrange("p (c e f) -> p c e f", c=C, e=E)
        moe_dn = arena_dn[0:F, :].rearrange("p (e d) -> p e d", e=E)
        x_res = sb("x_res", [P, T, D])
        h1T = sb("h1T", [P, C, N])
        shared = sb("shared", [P, 3072])
        sgu_w = shared[:, 0:2048].rearrange("p (c n) -> p c n", c=C)
        sd_w = shared[:, 2048:3072].rearrange("p (f n) -> p f n", f=SH // P)
        attn_w = sb("attn_w", [P, 4, C, D])
        mx_w = sb("mx_w", [P, 6144])
        mx_gu = arena_dn[:, 0:4096].rearrange("p (c n) -> p c n", c=C)
        mx_dn = arena_dn[:, 4096:6144].rearrange("p (i n) -> p i n", i=INNER // P)
        w_nat = mx_w[:, 0:2048].rearrange("p (w o n) -> p w o n", w=4, o=C)
        hs = mx_w[:, 0:4096].rearrange("p (f n) -> p f n", f=SH // P)
        router_sb = sb("router_sb", [P, C, E])
        rbias = sb("rbias", [P, E])
        bias_bc = sb("bias_bc", [P, 6, D])
        QB_, KB_, VB_, OB_, NQ_, NK_ = range(6)
        gates = sb("gates", [P, 4])
        tg = sb("tg", [P, 4])
        GX0, GX1, GF0, GF1 = range(4)
        ident = sb("ident", [P, P])
        tri = sb("tri", [P, P], BF16)
        ones = sb("ones", [P, P], BF16)
        iota = sb("iota", [P, P])
        pcol = sb("pcol", [P, 1])
        tokid = sb("tokid", [P, T])
        mhalf = sb("mhalf", [P, T])
        decay = sb("decay", [P, C])
        wdec = sb("wdec", [P, C])
        tdtf = sb("tdtf", [P, 2, C])
        negm = sb("negm", [P, C])
        umm = sb("umm", [P, C])
        stats = sb("stats", [P, T, 6])
        mv = sb("mv", [P, T, 2])
        rstd = sb("rstd", [P, T])
        macc = sb("macc", [P, 2, E], BF16)
        combs = sb("combs", [P, T, K])
        rank_all = sb("rank_all", [P, T, K])
        slot_u = sb("slot_u", [P, T * K], U32)
        tokf = sb("tokf", [P, NB])
        eid_row = sb("eid_row", [1, P], I32)

        def carver(region, at=0):
            state = [at]

            def take(*shape, dt=F32):
                n = 1
                for s in shape:
                    n *= s
                words = (n + 1) // 2 if dt in (F16, BF16) else n
                words = (words + 7) // 8 * 8
                a = region[:, state[0]:state[0] + words]
                state[0] += words
                assert state[0] <= region.shape[1], state[0]
                if dt != F32:
                    a = a.bitcast(dt)
                a = a[:, 0:n]
                if len(shape) == 1:
                    return a
                names = "abcd"[:len(shape)]
                return a.rearrange(f"p ({' '.join(names)}) -> p {' '.join(names)}",
                                   **dict(zip(names[:-1], shape)))
            return take

        take = carver(arena_dn, E * D // 2)
        A = 2
        xnA = [take(D) for _ in range(A)]
        cxA = [take(D) for _ in range(A)]
        ekm = [take(C, P) for _ in range(A)]
        eku = [take(C, P) for _ in range(A)]
        vTs = [take(C, P) for _ in range(A)]
        pm = [take(C, P) for _ in range(A)]
        pu = [take(C, P) for _ in range(A)]
        sA = [take(C, P + 1) for _ in range(A)]
        sB = [take(C, P + 1) for _ in range(A)]
        num = [take(C, P) for _ in range(A)]
        den = [take(C, P) for _ in range(A)]
        yA = [take(C, P) for _ in range(A)]

        take = carver(arena_dn, E * D // 2)
        onehot = take(T, K, E, dt=BF16)
        tmp = take(T * K, E)
        sgt = [take(512) for _ in range(2)]
        upt = [take(512) for _ in range(2)]
        h1B = [take(D) for _ in range(2)]
        h1S = mx_w[:, 4096:6144].rearrange("p (t d) -> p t d", t=T)
        h1Ts = [take(C, P) for _ in range(2)]
        biased = [take(E) for _ in range(2)]
        pexp = [take(E) for _ in range(2)]
        mask = [take(E, dt=BF16) for _ in range(2)]
        nmx = [take(1) for _ in range(2)]
        v8 = take(8)
        i8 = take(8, dt=U32)
        i8f = take(8)
        ck = take(K)
        cs = take(1)
        rcs = take(1)
        prod = take(K, E)
        prod2 = take(K, E)
        cnt_i = take(E, dt=I32)
        nb_i = take(E, dt=I32)
        nbf = take(E)
        cum = take(E)
        base = take(E)
        cmp = take(E)
        eidf = take(1)
        eidm = take(1)
        sbase = take(T * K)
        slotf = take(T * K)
        slot_i = take(T * K, dt=I32)
        blk_i = take(T * K, dt=I32)
        pos_i = take(T * K, dt=I32)
        blkf = take(T * K)
        posf = take(T * K)
        poh = [take(P, dt=F16) for _ in range(4)]
        boh = [take(NB, dt=F16) for _ in range(4)]

        take = carver(shared)
        xg = [take(2, D) for _ in range(4)]
        xgT = [take(2, C, P) for _ in range(2)]
        take = carver(h1T[:, :, :].rearrange("p c n -> p (c n)"))
        sgb = [take(2, F) for _ in range(2)]
        hb = [take(2, F) for _ in range(2)]
        hbT = [take(2, P) for _ in range(2)]
        ysb = [take(2, D) for _ in range(2)]
        gidx = sb("gidx", [P, 8], U32)

        take = carver(arena_up)
        yk = [[take(D) for _ in range(K)] for _ in range(2)]
        xnE = [take(D) for _ in range(2)]
        cxE = [take(D) for _ in range(2)]
        xTE = [take(C, P) for _ in range(2)]
        cTE = [take(C, P) for _ in range(2)]
        qb = [take(D) for _ in range(2)]
        kb = [take(D) for _ in range(2)]
        sq = [take(D) for _ in range(2)]
        ssq = [take(2) for _ in range(2)]
        rq = [take(2) for _ in range(2)]
        qn = [take(H, HP) for _ in range(2)]
        kn = [take(H, HP) for _ in range(2)]
        qT = [take(4, P) for _ in range(2)]
        kT = [take(4, P) for _ in range(2)]
        va = [take(H, HD + 1) for _ in range(2)]
        smax = [take(H) for _ in range(2)]
        sS = take(4, 4, P)
        pT = take(4, 4, P)
        rsum = [take(H) for _ in range(2)]
        oE = [take(H, HD) for _ in range(2)]
        oT = [take(C, P) for _ in range(2)]
        gob = take(D)

        take = carver(arena_dn, 6144)
        xnF = [take(D) for _ in range(2)]
        xyF = take(D)
        xeF = take(D)
        xaF = take(D)
        xqF = [take(D) for _ in range(2)]
        xTF = [take(C, P) for _ in range(2)]
        amx = take(8)
        amc = take(8)
        arc = take(8)
        HW = INNER // 2
        amh = [take(HW // QB) for _ in range(2)]
        ahc = [take(HW // QB) for _ in range(2)]
        ahr = [take(HW // QB) for _ in range(2)]
        sgF = [take(HW) for _ in range(2)]
        hF = [take(HW) for _ in range(2)]
        hyF = take(HW)
        heF = take(HW)
        haF = [take(HW) for _ in range(2)]
        take = carver(mx_w)
        hqF = [take(INNER) for _ in range(2)]
        hTF = [take(8, P) for _ in range(2)]
        WC = 256
        NWC = 6144 // WC
        we = sb("we", [P, WC])
        wam = sb("wam", [P, WC // QB])
        wac = sb("wac", [P, WC // QB])
        war = sb("war", [P, WC // QB])

        small = sb("small", [P, 16])
        epsc = sb("epsc", [P, 2])
        epsr = sb("epsr", [P, 2])
        eidx = sb("eidx", [P, 8], U32)

        gate_v = gate_w.rearrange("(n p) d -> p n d", p=P)
        up_v = up_w.rearrange("(n p) d -> p n d", p=P)
        down_v = down_w.rearrange("(n p) d -> p n d", p=P)

        block = ctx.enter_context(nc.Block())

        @block.sync
        def _(sp):
            def cxA_load(at):
                i = at(0)
                reach(sp, sem("kvT"), i.n - 1)
                sp.dma_start(cxA[i.slot], ctx_in[i.n]).then_inc(sem(f"cxA_in{i.slot}"), 16)

            sp.dma_start(x_res[:, :, :], x.rearrange("t p d -> p t d")).then_inc(sem("x_in"), 16)
            small_in = [(tdtf[:, 0, :], time_decay.rearrange("(c p) -> p c", p=P)),
                        (tdtf[:, 1, :], time_first.rearrange("(c p) -> p c", p=P)),
                        (gates[:, 0:2], g_xattn.partition_broadcast(P)),
                        (gates[:, 2:4], g_ffn.partition_broadcast(P)),
                        (router_sb[:, :, :], router_w.rearrange("(c p) e -> p c e", p=P)),
                        (rbias[:, :], router_bias.partition_broadcast(P))]
            small_in += [(bias_bc[:, n, :], v.partition_broadcast(P))
                         for n, v in enumerate((q_b, k_b, v_b, o_b, norm_q_w, norm_k_w))]
            for dst, src in small_in:
                sp.dma_start(dst, src, allow_slow_non_contiguous=True).then_inc(sem("small_in"), 16)
            for n, w in enumerate((q_w, k_w, v_w, o_w)):
                sp.dma_start(w_nat[:, n, :, :], w.rearrange("(o p) n -> p o n", p=P)).then_inc(sem("wnat_in"), 16)
            run_steps(sp, T, 0, 2, cxA_load)
            for s in range(2):
                for k, w in enumerate((swg, swu)):
                    sp.dma_start(sgu_w[:, :, k * SH + s * D:k * SH + (s + 1) * D],
                                 w[s].rearrange("(c p) n -> p c n", p=P)).then_inc(sem("shared_in"), 16)
                sp.dma_start(sd_w[:, 2 * s:2 * s + 2, :],
                             swd[s].rearrange("(f p) n -> p f n", p=P)).then_inc(sem("shared_in"), 16)
            for c in range(C):
                for n, w in enumerate((wg, wu)):
                    for e in range(0, E, 16):
                        sp.dma_start(moe_up[:, c, e:e + 16, n * F:(n + 1) * F],
                                     w[e:e + 16, c * P:(c + 1) * P, :].rearrange("e p f -> p e f"))\
                          .then_inc(sem("moe_in"), 16)
            for e in range(0, E // 2, 16):
                sp.dma_start(moe_dn[:, e:e + 16, :], wd[e:e + 16].rearrange("e f d -> f e d"))\
                  .then_inc(sem("moe_in"), 16)

            def h1_store(at):
                i = at(0)
                sp.wait_ge(sem("h1S"), i.n + 1)
                sp.dma_start(h1_dram[bass.ds(i.n * P, P), :], h1S[:, i.n, :]).then_inc(sem(f"h1_out{i.slot}"), 16)
            run_steps(sp, T, 0, 2, h1_store)
            sp.wait_ge(sem("tok"), 1)
            for b in range(2):
                sp.wait_ge(sem(f"h1_out{b}"), 16 * (T // 2))
            sp.wait_ge(sem("hs"), 8)
            for e in range(E // 2, E, 16):
                sp.dma_start(moe_dn[:, e:e + 16, :], wd[e:e + 16].rearrange("e f d -> f e d"))\
                  .then_inc(sem("moe_in2"), 16)

            sp.wait_ge(sem("xgT_ps"), 2)
            for n, w in enumerate((gate_v, up_v)):
                sp.dma_start(mx_w[:, n * 2048:(n + 1) * 2048].rearrange("p (r k) -> p r k", r=8), w)\
                  .then_inc(sem("mx_in"), 16)
            sp.dma_start(mx_w[:, 4096:6144].rearrange("p (r k) -> p r k", r=2), down_v).then_inc(sem("mx_in"), 16)

            def ys_store(at):
                i = at(0)
                sp.wait_ge(sem("ysb"), i.n + 1)
                sp.dma_start(ys_dram[bass.ds(i.n * 2 * P, 2 * P), :].rearrange("(b p) d -> p b d", p=P),
                             ysb[i.slot]).then_inc(sem(f"ys_out{i.slot}"), 16)
            run_steps(sp, NB // 2, 0, 2, ys_store)
            sp.wait_ge(sem("gu"), NB // 2)

            def cxE_load(at):
                i = at(0)
                if not (isinstance(i.n, int) and i.n < 2):
                    sp.wait_ge(sem("cTE_ps"), i.n - 1)
                sp.dma_start(cxE[i.slot], ctx_in[i.n]).then_inc(sem(f"cxE_in{i.slot}"), 16)
            run_steps(sp, T, 0, 2, cxE_load)
            def out_store(at):
                i = at(0)
                sp.wait_ge(sem("x4"), i.n + 1)
                sp.dma_start(out[i.n], x_res[:, i.n, :]).then_inc(sem("out_done"), 16)
            run_steps(sp, T, 0, 2, out_store)
            sp.wait_ge(sem("out_done"), 16 * T)

        @block.gpsimd
        def _(pool):
            pool.memset(ident[:, :], 0.0).then_inc(sem("cz"), 1)
            pool.memset(tri[:, :], 1.0).then_inc(sem("cz"), 1)
            pool.memset(ones[:, :], 1.0).then_inc(sem("const"), 1)
            pool.memset(mhalf[:, :], -0.5).then_inc(sem("const"), 1)
            pool.memset(epsc[:, :], LN_EPS).then_inc(sem("const"), 1)
            pool.memset(epsr[:, :], D * RMS_EPS).then_inc(sem("const"), 1)
            pool.memset(macc[:, 0, :], 0.0).then_inc(sem("const"), 1)
            pool.iota(iota[:, :], [[1, P]], base=0, channel_multiplier=0,
                      allow_small_or_imprecise_dtypes=True).then_inc(sem("const"), 1)
            pool.iota(pcol[:, :], [[0, 1]], base=0, channel_multiplier=1,
                      allow_small_or_imprecise_dtypes=True).then_inc(sem("const"), 1)
            pool.iota(tokid[:, :], [[P, T]], base=0, channel_multiplier=1,
                      allow_small_or_imprecise_dtypes=True).then_inc(sem("const"), 1)
            for b in range(A):
                for s in (sA, sB):
                    pool.memset(s[b][:, :, 0:1], 0.0).then_inc(sem("const"), 1)
            pool.wait_ge(sem("cz"), 2)
            pool.affine_select(out=ident[:, :], in_=ident[:, :], compare_op=ALU.not_equal, fill=1.0,
                               base=0, pattern=[[-1, P]], channel_multiplier=1).then_inc(sem("const"), 1)
            pool.affine_select(out=tri[:, :], in_=tri[:, :], compare_op=ALU.is_gt, fill=0.0,
                               base=0, pattern=[[1, P]], channel_multiplier=-1).then_inc(sem("const"), 1)
            CONST = 14

            def inv_sqrt(dst, src, scale, eps, temp, ready, value, done):
                pool.wait_ge(sem(ready), value)
                pool.tensor_scalar(temp, src, scale, eps, ALU.mult, ALU.add).then_inc(sem("isq"), 1)
                isq[0] = isq[0] + 1
                pool.wait_ge(sem("isq"), isq[0])
                pool.tensor_tensor(dst, temp, mhalf[:, 0:temp.shape[1]], ALU.pow).then_inc(sem(done), 1)

            isq = [0]
            pool.wait_ge(sem("const"), CONST)
            inv_sqrt(rstd[:, :], mv[:, :, 1], 1.0, LN_EPS, small[:, 0:T], "mv", T, "rstd")

            def wkv_sums(at):
                i = at(0)
                if i is None:
                    return
                n = i.n
                pool.wait_ge(sem("exps"), n + 1)
                pool.wait_ge(sem("vTs"), n + 1)
                reach(pool, sem("yA"), n - 1)
                pool.tensor_tensor(pu[i.slot], eku[i.slot], vTs[i.slot], ALU.mult).then_inc(sem("pu"), 1)
                pool.wait_ge(sem("scan"), n + 1)
                pool.tensor_tensor(den[i.slot], sB[i.slot][:, :, 0:P], eku[i.slot], ALU.add)
                pool.wait_ge(sem("pu"), n + 1)
                pool.tensor_tensor(num[i.slot], sA[i.slot][:, :, 0:P], pu[i.slot], ALU.add)\
                    .then_inc(sem("numden"), 1)
            run_steps(pool, T, 0, 2, wkv_sums)

            def route_pool(at):
                i = at(0)
                if i is not None:
                    pool.wait_ge(sem("mvB"), i.n + 1)
                    pool.tensor_tensor(small[:, 8 + i.slot:9 + i.slot], mv[:, i.slot, 1:2], epsc[:, 0:1], ALU.add).then_inc(sem("isqB"), 1)
                    pool.wait_ge(sem("isqB"), i.n + 1)
                    pool.tensor_tensor(rstd[:, i.slot:i.slot + 1], small[:, 8 + i.slot:9 + i.slot],
                                       mhalf[:, 0:1], ALU.pow).then_inc(sem("rstdB"), 1)
                    pool.wait_ge(sem("h1"), i.n + 1)
                    pool.tensor_copy(h1S[:, i.n, :], h1B[i.slot]).then_inc(sem("h1S"), 1)
                i = at(1)
                if i is not None:
                    pool.wait_ge(sem("h1T"), i.n + 1)
                    pool.tensor_copy(h1T[:, :, bass.ds(i.n * P, P)], h1Ts[i.slot]).then_inc(sem("h1T_all"), 1)
                i = at(2)
                if i is not None:
                    pool.wait_ge(sem("mask"), i.n + 1)
                    reach(pool, sem("rank"), i.n)
                    reach(pool, sem("macc"), i.n)
                    pool.tensor_tensor(macc[:, 1 - i.slot, :], macc[:, i.slot, :], mask[i.slot], ALU.add)\
                        .then_inc(sem("macc"), 1)
            run_steps(pool, T, 2, 2, route_pool, lead=2)

            for n in range(8):
                f, hf = n % 4, n // 4
                pool.wait_ge(sem("sgt"), n + 1)
                pool.tensor_tensor(hs[:, f, hf * 512:(hf + 1) * 512], sgt[n % 2], upt[n % 2], ALU.mult)\
                    .then_inc(sem("hs"), 1)

            pool.wait_ge(sem("tok"), 1)
            for b in range(2):
                pool.wait_ge(sem(f"h1_out{b}"), 16 * (T // 2))
            pool.wait_ge(sem("sdown"), 8)

            def gather(at):
                i = at(0)
                q = 2 * i.slot
                reach(pool, sem("xgT_ps"), i.n - 3)
                pool.tensor_copy(gidx[:, q:q + 2], tokf[:, bass.ds(2 * i.n, 2)]).then_inc(sem("gidx"), 1)
                wait_apart(pool, (sem("tok"), 1), (sem("gidx"), i.n + 1))
                for b in range(2):
                    pool.indirect_dma_start(out=xg[i.slot][:, b, :], out_offset=None, in_=h1_dram[:, :],
                                            in_offset=bass.IndirectOffsetOnAxis(ap=gidx[:, q + b:q + b + 1], axis=0))\
                        .then_inc(sem(f"xg{i.slot}"), 16)
            run_steps(pool, NB // 2, 0, 4, gather)

            for b in range(2):
                pool.wait_ge(sem(f"ys_out{b}"), 16 * (NB // 4))
            pool.wait_ge(sem("gu"), NB // 2)
            for b in range(2):
                pool.memset(qn[b][:, :, HD:HP], 0.0).then_inc(sem("padE"), 1)
                pool.memset(kn[b][:, :, HD:HP], 0.0).then_inc(sem("padE"), 1)
                pool.memset(va[b][:, :, HD:HD + 1], 1.0).then_inc(sem("padE"), 1)

            def combine(at):
                i = at(0)
                if i is not None:
                    if not (isinstance(i.n, int) and i.n < 2):
                        pool.wait_ge(sem("x2"), i.n - 1)
                    pool.tensor_copy(eidx[:, 4 * i.slot:4 * i.slot + 4], slot_u[:, bass.ds(i.n * K, K)])\
                        .then_inc(sem("eidx"), 1)
                    wait_apart(pool, (sem("tok"), 1), (sem("eidx"), i.n + 1))
                    for k in range(K):
                        pool.indirect_dma_start(
                            out=yk[i.slot][k], out_offset=None, in_=ys_dram[:, :],
                            in_offset=bass.IndirectOffsetOnAxis(ap=eidx[:, 4 * i.slot + k:4 * i.slot + k + 1], axis=0))\
                            .then_inc(sem(f"yk{i.slot}"), 16)
                i = at(2)
                if i is not None:
                    s = i.slot
                    pool.wait_ge(sem("ssq"), i.n + 1)
                    pool.tensor_tensor(small[:, 4 + 2 * s:6 + 2 * s], ssq[s], epsr[:, :], ALU.add)\
                        .then_inc(sem("isqQ"), 1)
                    pool.wait_ge(sem("isqQ"), i.n + 1)
                    pool.tensor_tensor(rq[s], small[:, 4 + 2 * s:6 + 2 * s], mhalf[:, 0:2], ALU.pow)\
                        .then_inc(sem("rq"), 1)
                i = at(1)
                if i is not None:
                    s = i.slot
                    pool.wait_ge(sem("mvE"), i.n + 1)
                    pool.tensor_tensor(small[:, s:s + 1], mv[:, s, 1:2], epsc[:, 0:1], ALU.add)\
                        .then_inc(sem("isqE"), 1)
                    pool.wait_ge(sem("isqE"), i.n + 1)
                    pool.tensor_tensor(rstd[:, s:s + 1], small[:, s:s + 1], mhalf[:, 0:1], ALU.pow)\
                        .then_inc(sem("rstdE"), 1)
            run_steps(pool, T, 2, 2, combine, lead=2)

            def ffn_pool(at):
                i = at(0)
                if i is not None:
                    s = i.slot
                    pool.wait_ge(sem("mvF"), i.n + 1)
                    pool.tensor_tensor(small[:, s:s + 1], mv[:, s, 1:2], epsc[:, 0:1], ALU.add)\
                        .then_inc(sem("isqF"), 1)
                    pool.wait_ge(sem("isqF"), i.n + 1)
                    pool.tensor_tensor(rstd[:, s:s + 1], small[:, s:s + 1], mhalf[:, 0:1], ALU.pow)\
                        .then_inc(sem("rstdF"), 1)
                i = at(2)
                if i is not None:
                    for h in range(2):
                        pool.wait_ge(sem("hround"), 2 * i.n + h + 1)
                        reach(pool, sem("hTF_ps"), 2 * i.n + h - 3)
                        pool.tensor_tensor(hqF[i.slot][:, h * HW:(h + 1) * HW].rearrange("p (b w) -> p b w", w=QB),
                                           haF[h].rearrange("p (b w) -> p b w", w=QB),
                                           ahc[h].unsqueeze(2).to_broadcast([P, HW // QB, QB]), ALU.mult)\
                            .then_inc(sem("hqF"), 1)
            run_steps(pool, T, 2, 2, ffn_pool, lead=2)

        @block.scalar
        def _(act):
            act.wait_ge(sem("small_in"), 16 * 12)
            act.activation(tg[:, :], gates[:, :], ACT.Tanh).then_inc(sem("tg"), 1)
            act.activation(wdec[:, :], tdtf[:, 0, :], ACT.Exp).then_inc(sem("wdec"), 1)
            act.wait_ge(sem("wdec"), 1)
            act.activation(decay[:, :], wdec[:, :], ACT.Exp, scale=-1.0).then_inc(sem("decay"), 1)
            for n in range(8):
                act.wait_ge(sem("wT_ps"), n + 1)
                act.copy(attn_w[:, n // 2, n % 2, :], bank[6 + n % 2][:, 0:D]).then_inc(sem("wT"), 1)
            act.wait_ge(sem("negm"), 1)

            def wkv_exps(at):
                i = at(0)
                if i is None:
                    return
                n, s = i.n, i.slot
                act.wait_ge(sem("kvT"), n + 1)
                reach(act, sem("numden"), n - 1)
                reach(act, sem("yA"), n - 1)
                for c in range(C):
                    act.activation(ekm[s][:, c, :], bank[s][:, c * P:(c + 1) * P], ACT.Exp, bias=negm[:, c:c + 1])
                    ins = act.activation(eku[s][:, c, :], bank[s][:, c * P:(c + 1) * P], ACT.Exp,
                                         bias=umm[:, c:c + 1])
                ins.then_inc(sem("exps"), 1)
                act.copy(vTs[s], bank[2 + s][:, 0:D].rearrange("p (c n) -> p c n", c=C)).then_inc(sem("vTs"), 1)
            run_steps(act, T, 0, 2, wkv_exps)

            def route_act(at):
                i = at(0)
                if i is not None:
                    act.wait_ge(sem("h1T_ps"), i.n + 1)
                    reach(act, sem("h1T_all"), i.n - 1)
                    reach(act, sem("logits"), i.n - 1)
                    act.copy(h1Ts[i.slot], bank[i.slot][:, 0:D].rearrange("p (c n) -> p c n", c=C))\
                        .then_inc(sem("h1T"), 1)
                i = at(1)
                if i is not None:
                    act.wait_ge(sem("biased"), i.n + 1)
                    reach(act, sem("ck"), i.n - 1)
                    act.activation(pexp[i.slot], bank[2 + i.slot][:, 0:E], ACT.Exp, bias=nmx[i.slot])\
                        .then_inc(sem("pexp"), 1)
            run_steps(act, T, 1, 2, route_act)
            for n in range(8):
                act.wait_ge(sem("sup_ps"), n + 1)
                reach(act, sem("hs"), n - 1)
                act.activation(sgt[n % 2], bank[n % 2][:, :], ACT.Silu)
                act.copy(upt[n % 2], bank[2 + n % 2][:, :]).then_inc(sem("sgt"), 1)

            def moe_act(at):
                i = at(1)
                if i is not None:
                    for p in range(2):
                        act.wait_ge(sem("gu"), 2 * i.n + p + 1)
                        reach(act, sem("hb"), 2 * i.n + p - 1)
                        act.activation(sgb[p], bank[2 + p][:, 0:4 * F].rearrange("p (b n f) -> p b n f", b=2, n=2)[:, :, 0, :],
                                       ACT.Silu).then_inc(sem("sgb"), 1)
                i = at(0)
                if i is not None:
                    for p in range(2):
                        act.wait_ge(sem("xgT_ps"), 2 * i.n + p + 1)
                        reach(act, sem("gu"), 2 * i.n + p - 1)
                        act.copy(xgT[p], bank[p][:, :].rearrange("p (b c n) -> p b c n", b=2, c=C))\
                            .then_inc(sem("xgT"), 1)
            run_steps(act, NB // 4, 1, 2, moe_act)

            def mx_copies():
                for n in range(12):
                    act.wait_ge(sem("mxT_ps"), n + 1)
                    src = bank[6 + n % 2][:, :]
                    if n < 8:
                        dst = mx_gu[:, :, n * 256:(n + 1) * 256].rearrange("p c (r o) -> p r c o", r=2)
                        act.copy(dst, src.rearrange("p (r c o) -> p r c o", r=2, c=C)).then_inc(sem("mxT"), 1)
                    else:
                        r, q4 = (n - 8) // 2, (n - 8) % 2
                        dst = mx_dn[:, 4 * q4:4 * q4 + 4, r * P:(r + 1) * P]
                        act.copy(dst, src.rearrange("p (i o) -> p i o", i=4)).then_inc(sem("mxT"), 1)

            def attn_act(at):
                front, mid, back = at(0), at(1), at(2)

                def square_q():
                    if mid is not None:
                        act.wait_ge(sem("qb"), mid.n + 1)
                        act.activation(sq[0], qb[mid.slot], ACT.Square, accum_out=ssq[mid.slot][:, 0:1])\
                            .then_inc(sem("ssq"), 1)

                if back is not None:
                    for j in range(4):
                        act.wait_ge(sem("shift"), 4 * back.n + j + 1)
                        act.activation(sS[:, j, :, :], sS[:, j, :, :], ACT.Exp).then_inc(sem("probs"), 1)
                if mid is not None:
                    n, s = mid.n, mid.slot
                    act.wait_ge(sem("kb"), n + 1)
                    reach(act, sem("rq"), n - 1)
                    act.activation(sq[1], kb[s], ACT.Square, accum_out=ssq[s][:, 1:2]).then_inc(sem("sq"), 1)
                if back is not None:
                    n = back.n
                    for j in range(4):
                        act.wait_ge(sem("pT_ps"), 4 * n + j + 1)
                        if j == 0:
                            reach(act, sem("pv"), n)
                        act.copy(pT[:, j, :, :], bank[6 + j % 2][:, :].rearrange("p (g n) -> p g n", g=4))\
                            .then_inc(sem("pT"), 1)
                        if j == 0:
                            square_q()
                elif mid is not None:
                    square_q()
                    mx_copies()
                if mid is not None:
                    n, s = mid.n, mid.slot
                    act.wait_ge(sem("qT_ps"), n + 1)
                    reach(act, sem("S"), n - 1)
                    act.copy(qT[s], bank[1][:, :].rearrange("p (g n) -> p g n", g=4)).then_inc(sem("qT"), 1)
                    act.wait_ge(sem("kT_ps"), n + 1)
                    act.copy(kT[s], bank[0][:, :].rearrange("p (g n) -> p g n", g=4)).then_inc(sem("kT"), 1)
                if back is not None:
                    n, s = back.n, back.slot
                    act.wait_ge(sem("oT_ps"), n + 1)
                    reach(act, sem("o_ps"), n - 1)
                    act.copy(oT[s], bank[5][:, 0:D].rearrange("p (c n) -> p c n", c=C)).then_inc(sem("oT"), 1)
                if front is not None:
                    n, s = front.n, front.slot
                    act.wait_ge(sem("cTE_ps"), n + 1)
                    reach(act, sem("kv_ps"), n - 1)
                    act.copy(cTE[s], bank[2][:, 0:D].rearrange("p (c n) -> p c n", c=C)).then_inc(sem("cTE"), 1)
                    act.wait_ge(sem("xTE_ps"), n + 1)
                    reach(act, sem("q_ps"), n - 1)
                    act.copy(xTE[s], bank[3][:, 0:D].rearrange("p (c n) -> p c n", c=C)).then_inc(sem("xTE"), 1)
            run_steps(act, T, 2, 2, attn_act, lead=2)

            def ffn_act(at):
                i = at(0)
                if i is not None:
                    n, s = i.n, i.slot
                    act.wait_ge(sem("xTF_ps"), n + 1)
                    reach(act, sem("gu8"), 4 * n - 4)
                    act.copy(xTF[s], bank[0][:, 0:D].rearrange("p (c n) -> p c n", c=C)).then_inc(sem("xTF"), 1)
                    for h in range(2):
                        act.wait_ge(sem("gu8"), 4 * n + 2 * h + 1)
                        reach(act, sem("hF"), 2 * n + h - 1)
                        act.activation(sgF[h], bank[2 + h][:, :], ACT.Silu).then_inc(sem("sgF"), 1)
                i = at(1)
                if i is not None:
                    n, s = i.n, i.slot
                    for h in range(2):
                        act.wait_ge(sem("hTF_ps"), 2 * n + h + 1)
                        reach(act, sem("dF"), n - 1)
                        act.copy(hTF[s][:, 4 * h:4 * h + 4, :], bank[6 + h][:, :].rearrange("p (i n) -> p i n", i=4))\
                            .then_inc(sem("hTF"), 1)
            run_steps(act, T, 1, 2, ffn_act)

        @block.vector
        def _(dve):
            count = {}

            def chain(ins, name):
                ins.then_inc(sem(name), 1)
                count[name] = count.get(name, 0) + 1
                dve.wait_ge(sem(name), count[name])

            dve.wait_ge(sem("small_in"), 16 * 12)
            chain(dve.tensor_scalar(negm[:, :], tdtf[:, 1, :], 0.0, -1.0, ALU.max, ALU.mult), "r")
            dve.tensor_tensor(umm[:, :], tdtf[:, 1, :], negm[:, :], ALU.add).then_inc(sem("negm"), 1)
            dve.wait_ge(sem("x_in"), 16)
            for t in range(T):
                ins = dve.bn_stats(stats[:, t, :], x_res[:, t, :])
            ins.then_inc(sem("st"), 1)
            dve.wait_ge(sem("st"), 1)
            for t in range(T):
                dve.bn_aggr(mv[:, t, :], stats[:, t, :]).then_inc(sem("mv"), 1)
            dve.wait_ge(sem("rstd"), 1)
            dve.wait_ge(sem("decay"), 1)
            dve.wait_ge(sem("tg"), 1)
            dve.wait_ge(sem("const"), 14)

            def wkv(at):
                i = at(0)
                if i is not None:
                    reach(dve, sem("kvT"), i.n - 1)
                    dve.tensor_scalar(xnA[i.slot], x_res[:, i.n, :], mv[:, i.n, 0:1], rstd[:, bass.ds(i.n, 1)],
                                      ALU.subtract, ALU.mult).then_inc(sem("xnA"), 1)
                i = at(1)
                if i is not None:
                    n, s = i.n, i.slot
                    dve.wait_ge(sem("exps"), n + 1)
                    dve.wait_ge(sem("vTs"), n + 1)
                    reach(dve, sem("scan"), n - 1)
                    reach(dve, sem("numden"), n - 1)
                    dve.tensor_tensor(pm[s], ekm[s], vTs[s], ALU.mult).then_inc(sem("pm"), 1)
                    dve.wait_ge(sem("pm"), n + 1)
                    for c in range(C):
                        d = decay[:, c:c + 1].to_broadcast([P, P])
                        dve.tensor_tensor_scan(sB[s][:, c, 1:P + 1], d, ekm[s][:, c, :], 0.0, ALU.mult, ALU.add)
                        ins = dve.tensor_tensor_scan(sA[s][:, c, 1:P + 1], d, pm[s][:, c, :], 0.0,
                                                     ALU.mult, ALU.add)
                    ins.then_inc(sem("scan"), 1)
                i = at(2)
                if i is not None:
                    n, s = i.n, i.slot
                    dve.wait_ge(sem("numden"), n + 1)
                    reach(dve, sem("yT_ps"), n - 1)
                    dve.reciprocal(den[s], den[s]).then_inc(sem("rden"), 1)
                    dve.wait_ge(sem("rden"), n + 1)
                    dve.tensor_tensor(yA[s], num[s], den[s], ALU.mult).then_inc(sem("ym"), 1)
                    dve.wait_ge(sem("ym"), n + 1)
                    dve.tensor_copy(yA[s][:, :, 0:1], vTs[s][:, :, 0:1]).then_inc(sem("yA"), 1)
                i = at(3)
                if i is not None:
                    dve.wait_ge(sem("yT_ps"), i.n + 1)
                    dve.scalar_tensor_tensor(x_res[:, i.n, :], bank[4 + i.slot][:, 0:D], tg[:, GX0:GX0 + 1],
                                             x_res[:, i.n, :], ALU.mult, ALU.add).then_inc(sem("x1"), 1)
            run_steps(dve, T, 3, 2, wkv, lead=2)

            def route(at):
                i = at(0)
                if i is not None:
                    n, s = i.n, i.slot
                    wait_apart(dve, (sem("const"), 14), (sem("x1"), n + 1), (sem("h1"), n - 1))
                    dve.bn_stats(stats[:, s, :], x_res[:, n, :]).then_inc(sem("stB"), 1)
                    wait_apart(dve, (sem("const"), 14), (sem("stB"), n + 1))
                    dve.bn_aggr(mv[:, s, :], stats[:, s, :]).then_inc(sem("mvB"), 1)
                i = at(1)
                if i is not None:
                    n, s = i.n, i.slot
                    dve.wait_ge(sem("rstdB"), n + 1)
                    dve.wait_ge(sem("mvB"), n + 1)
                    if not (isinstance(n, int) and n < 2):
                        dve.wait_ge(sem("h1S"), n - 1)
                        dve.wait_ge(sem("h1T_ps"), n - 1)
                    dve.tensor_scalar(h1B[s], x_res[:, n, :], mv[:, s, 0:1], rstd[:, s:s + 1],
                                      ALU.subtract, ALU.mult).then_inc(sem("h1"), 1)
                i = at(2)
                if i is not None:
                    n, s = i.n, i.slot
                    wait_apart(dve, (sem("const"), 14), (sem("logits"), n + 1), (sem("rc"), n - 1))
                    dve.tensor_reduce(nmx[s], bank[2 + s][:, 0:E], AX.X, ALU.max, negate=True)
                    dve.tensor_tensor(biased[s], bank[2 + s][:, 0:E], rbias[:, :], ALU.add).then_inc(sem("biased"), 1)
                    wait_apart(dve, (sem("const"), 14), (sem("biased"), n + 1))
                    dve.max(v8, biased[s]).then_inc(sem("pick"), 1)
                    wait_apart(dve, (sem("const"), 14), (sem("pick"), 4 * n + 1))
                    dve.max_index(i8, v8, biased[s]).then_inc(sem("pick"), 1)
                    dve.wait_ge(sem("pick"), 4 * n + 2)
                    dve.tensor_copy(i8f, i8).then_inc(sem("pick"), 1)
                    dve.wait_ge(sem("pick"), 4 * n + 3)
                    dve.tensor_tensor(onehot[:, n, :, :], iota[:, 0:E].unsqueeze(1).to_broadcast([P, K, E]),
                                      i8f[:, 0:K].unsqueeze(2).to_broadcast([P, K, E]), ALU.is_equal)\
                        .then_inc(sem("pick"), 1)
                    wait_apart(dve, (sem("const"), 14), (sem("pick"), 4 * n + 4), (sem("macc"), n - 1), (sem("rank"), n - 1))
                    with nc.allow_low_precision("counts of at most 8 are exact in bfloat16"):
                        dve.tensor_reduce(mask[s], onehot[:, n, :, :].rearrange("p k e -> p e k"), AX.X, ALU.add)\
                            .then_inc(sem("mask"), 1)
                i = at(3)
                if i is not None:
                    n, s = i.n, i.slot
                    dve.wait_ge(sem("pexp"), n + 1)
                    dve.tensor_tensor(prod, onehot[:, n, :, :], pexp[s].unsqueeze(1).to_broadcast([P, K, E]), ALU.mult)
                    dve.wait_ge(sem("rank"), n + 1)
                    dve.tensor_tensor(prod2, onehot[:, n, :, :],
                                      bank[4 + s][:, 0:E].unsqueeze(1).to_broadcast([P, K, E]), ALU.mult)\
                        .then_inc(sem("prod"), 1)
                    wait_apart(dve, (sem("const"), 14), (sem("prod"), n + 1))
                    dve.tensor_reduce(ck, prod, AX.X, ALU.add).then_inc(sem("ck"), 1)
                    dve.tensor_reduce(rank_all[:, n, :], prod2, AX.X, ALU.add)
                    wait_apart(dve, (sem("const"), 14), (sem("ck"), n + 1))
                    dve.tensor_reduce(cs, ck, AX.X, ALU.add).then_inc(sem("share"), 1)
                    dve.wait_ge(sem("share"), 2 * n + 1)
                    dve.reciprocal(rcs, cs).then_inc(sem("share"), 1)
                    dve.wait_ge(sem("share"), 2 * n + 2)
                    dve.tensor_scalar(combs[:, n, :], ck, rcs[:, 0:1], tg[:, GF0:GF0 + 1], ALU.mult, ALU.mult)\
                        .then_inc(sem("rc"), 1)
            run_steps(dve, T, 3, 2, route, lead=2)

            dve.wait_ge(sem("counts"), 1)
            chain(dve.tensor_scalar(cnt_i, bank[6][:, 0:E], float(P - 1), None, ALU.add), "r")
            chain(dve.tensor_scalar(nb_i, cnt_i, 7, None, ALU.logical_shift_right), "r")
            chain(dve.tensor_copy(nbf, nb_i), "r")
            chain(dve.tensor_tensor_scan(cum, ones[:, 0:E], nbf, 0.0, ALU.mult, ALU.add), "r")
            dve.tensor_scalar(cmp, cum, pcol[:, 0:1], None, ALU.is_le)
            chain(dve.tensor_tensor(base, cum, nbf, ALU.subtract), "r")
            chain(dve.tensor_reduce(eidf, cmp, AX.X, ALU.add), "r")
            dve.tensor_scalar(eidm, eidf, float(E - 1), None, ALU.min).then_inc(sem("eidm"), 1)
            chain(dve.tensor_scalar(base, base, float(P), None, ALU.mult), "r")
            chain(dve.tensor_tensor(tmp, onehot.rearrange("p t k e -> p (t k) e"),
                                    base.unsqueeze(1).to_broadcast([P, T * K, E]), ALU.mult), "r")
            chain(dve.tensor_reduce(sbase, tmp, AX.X, ALU.add), "r")
            chain(dve.tensor_tensor(slotf, sbase, rank_all[:, :, :].rearrange("p t k -> p (t k)"), ALU.add), "r")
            dve.tensor_copy(slot_u[:, :], slotf).then_inc(sem("slot_u"), 1)
            chain(dve.tensor_copy(slot_i, slotf), "r")
            dve.tensor_scalar(blk_i, slot_i, 7, None, ALU.logical_shift_right)
            chain(dve.tensor_scalar(pos_i, slot_i, P - 1, None, ALU.bitwise_and), "r")
            dve.tensor_copy(blkf, blk_i)
            chain(dve.tensor_copy(posf, pos_i), "r")
            dve.wait_ge(sem("eid_ps"), 1)
            dve.tensor_copy(eid_row[:, :], bank[7][0:1, 0:P]).then_inc(sem("eid"), 1)

            def table(at):
                i = at(0)
                if i is None:
                    return
                n, s = i.n, i.slot
                reach(dve, sem("tab_ps"), n - 3)
                dve.tensor_scalar(poh[s], iota[:, :], posf[:, bass.ds(n, 1)], None, ALU.is_equal)
                dve.tensor_scalar(boh[s], iota[:, 0:NB], blkf[:, bass.ds(n, 1)], tokid[:, bass.ds(i.lap, 1)],
                                  ALU.is_equal, ALU.mult).then_inc(sem("onehots"), 1)
            run_steps(dve, T * K, 0, 4, table)
            dve.wait_ge(sem("tab_ps"), T * K)
            dve.tensor_copy(tokf[:, :], bank[5][:, 0:NB]).then_inc(sem("tok"), 1)

            for t in range(T):
                dve.wait_ge(sem("sdown"), t + 1)
                dve.scalar_tensor_tensor(x_res[:, t, :], bank[2 + t % 2][:, 0:D], tg[:, GF0:GF0 + 1],
                                         x_res[:, t, :], ALU.mult, ALU.add).then_inc(sem("xs"), 1)

            def quantise(src, width, mx, sc, rs, y, e, a, name, before, last=None):
                nblk = width // QB
                b3 = "p (b w) -> p b w"

                def link(ins, k):
                    ins.then_inc(sem(name), 1)
                    dve.wait_ge(sem(name), before + k)
                link(dve.tensor_reduce(mx, src.rearrange(b3, w=QB), AX.X, ALU.max, apply_absolute_value=True), 1)
                link(dve.tensor_scalar(sc, mx, 1.0 / FP8_MAX, 1e-30, ALU.mult, ALU.max), 2)
                link(dve.reciprocal(rs, sc), 3)
                link(dve.tensor_tensor(y.rearrange(b3, w=QB), src.rearrange(b3, w=QB),
                                       rs.unsqueeze(2).to_broadcast([P, nblk, QB]), ALU.mult), 4)
                link(dve.tensor_scalar(e.bitcast(U32), y.bitcast(U32), EXPONENT, None, ALU.bitwise_and), 5)
                link(dve.tensor_scalar(e, e, FP8_TINY, ROUND4, ALU.max, ALU.mult), 6)
                link(dve.tensor_tensor(a, y, e, ALU.add), 7)
                ins = dve.tensor_tensor(a, a, e, ALU.subtract)
                if last is None:
                    link(ins, 8)
                else:
                    ins.then_inc(sem(last), 1)

            def rescale(dst, a, sc):
                b3 = "p (b w) -> p b w"
                a3 = a.rearrange(b3, w=QB)
                return dve.tensor_tensor(dst.rearrange(b3, w=QB), a3, sc.unsqueeze(2).to_broadcast(list(a3.shape)),
                                         ALU.mult)

            def weight_chunk(i):
                if i is None:
                    return
                if isinstance(i.n, int) and i.n == 0:
                    dve.wait_ge(sem("mx_in"), 3 * 16)
                w = mx_w[:, bass.ds(i.n * WC, WC)]
                wait_apart(dve, (sem("const"), 14), (sem("w_deq"), i.n))
                quantise(w, WC, wam[:, :], wac[:, :], war[:, :], w, we[:, :], w, "quantw", 8 * i.n)
                rescale(w, w, wac[:, :]).then_inc(sem("w_deq"), 1)

            def moe_dve(at):
                weight_chunk(at(4))
                if at(0) is None:
                    return
                i = at(0)
                for p in range(2):
                    dve.wait_ge(sem("sgb"), 2 * i.n + p + 1)
                    reach(dve, sem("hT_ps"), 2 * i.n + p - 1)
                    dve.tensor_tensor(hb[p], bank[2 + p][:, 0:4 * F].rearrange("p (b n f) -> p b n f", b=2, n=2)[:, :, 1, :],
                                      sgb[p], ALU.mult).then_inc(sem("hb"), 1)
                for p in range(2):
                    dve.wait_ge(sem("hT_ps"), 2 * i.n + p + 1)
                    reach(dve, sem("mo_y"), 2 * i.n + p - 1)
                    dve.tensor_copy(hbT[p][0:F, :, :], bank[4 + p][0:F, 0:2 * P].rearrange("p (b n) -> p b n", b=2))\
                        .then_inc(sem("hbT"), 1)
                for p in range(2):
                    dve.wait_ge(sem("mo_y"), 2 * i.n + p + 1)
                    reach(dve, sem(f"ys_out{p}"), 16 * i.n)
                    dve.tensor_copy(ysb[p], bank[6 + p][:, :].rearrange("p (b d) -> p b d", b=2)).then_inc(sem("ysb"), 1)
            run_steps(dve, NB // 4, 4, 2, moe_dve, lead=3)

            dve.wait_ge(sem("gu"), NB // 2)
            dve.wait_ge(sem("padE"), 6)
            dve.tensor_scalar(bias_bc[:, NQ_, :], bias_bc[:, NQ_, :], (D / HD) ** 0.5, None, ALU.mult)\
                .then_inc(sem("gob"), 1)
            dve.tensor_scalar(bias_bc[:, NK_, :], bias_bc[:, NK_, :], D ** 0.5, None, ALU.mult)\
                .then_inc(sem("gob"), 1)
            dve.tensor_scalar(gob, bias_bc[:, OB_, :], tg[:, GX1:GX1 + 1], None, ALU.mult).then_inc(sem("gob"), 1)
            dve.wait_ge(sem("gob"), 3)
            dve.wait_ge(sem("xs"), T)

            def attn(at):
                front, mid, back = at(0), at(1), at(2)
                if back is not None:
                    n, s = back.n, back.slot
                    reach(dve, sem("pT_ps"), 4 * n)
                    for j in range(4):
                        wait_apart(dve, (sem("const"), 14), (sem("S"), 4 * n + j + 1))
                        src = bank[j][:, :].rearrange("p (g k) -> p g k", g=4)
                        dve.tensor_reduce(smax[s][:, 4 * j:4 * j + 4], src, AX.X, ALU.max).then_inc(sem("smax"), 1)
                        dve.wait_ge(sem("smax"), 4 * n + j + 1)
                        dve.tensor_tensor(sS[:, j, :, :], src,
                                          smax[s][:, 4 * j:4 * j + 4].unsqueeze(2).to_broadcast([P, 4, P]),
                                          ALU.subtract).then_inc(sem("shift"), 1)
                if mid is not None:
                    n, s = mid.n, mid.slot
                    dve.wait_ge(sem("kv_ps"), n + 1)
                    reach(dve, sem("ssq"), n - 1)
                    dve.tensor_tensor(kb[s], bank[4][:, 0:D], bias_bc[:, KB_, :], ALU.add).then_inc(sem("kb"), 1)
                    reach(dve, sem("pv"), n - 1)
                    dve.tensor_tensor(va[s][:, :, 0:HD], bank[4][:, D:2 * D].rearrange("p (h d) -> p h d", h=H),
                                      bias_bc[:, VB_, :].rearrange("p (h d) -> p h d", h=H), ALU.add)\
                        .then_inc(sem("va"), 1)
                    dve.wait_ge(sem("q_ps"), n + 1)
                    dve.tensor_tensor(qb[s], bank[5][:, 0:D], bias_bc[:, QB_, :], ALU.add).then_inc(sem("qb"), 1)
                if front is not None:
                    n, s = front.n, front.slot
                    dve.wait_ge(sem(f"yk{s}"), 64 * (front.lap + 1))
                    for k in range(K):
                        dve.scalar_tensor_tensor(x_res[:, n, :], yk[s][k], combs[:, n, k:k + 1], x_res[:, n, :],
                                                 ALU.mult, ALU.add).then_inc(sem("x2k"), 1)
                        wait_apart(dve, (sem("const"), 14), (sem("x2k"), n * K + k + 1))
                    dve.bn_stats(stats[:, s, :], x_res[:, n, :]).then_inc(sem("x2"), 1)
                    wait_apart(dve, (sem("const"), 14), (sem("x2"), n + 1))
                    dve.bn_aggr(mv[:, s, :], stats[:, s, :]).then_inc(sem("mvE"), 1)
                if mid is not None:
                    n, s = mid.n, mid.slot
                    dve.wait_ge(sem("rq"), n + 1)
                    dve.wait_ge(sem("qb"), n + 1)
                    reach(dve, sem("kT_ps"), n - 1)
                    for raw, col, norm, dst, name in ((qb, 0, NQ_, qn, "qn"), (kb, 1, NK_, kn, "kn")):
                        dve.scalar_tensor_tensor(dst[s][:, :, 0:HD], raw[s].rearrange("p (h d) -> p h d", h=H),
                                                 rq[s][:, col:col + 1],
                                                 bias_bc[:, norm, :].rearrange("p (h d) -> p h d", h=H),
                                                 ALU.mult, ALU.mult).then_inc(sem(name), 1)
                if front is not None:
                    n, s = front.n, front.slot
                    dve.wait_ge(sem("rstdE"), n + 1)
                    dve.wait_ge(sem("mvE"), n + 1)
                    reach(dve, sem("xTE_ps"), n - 1)
                    dve.tensor_scalar(xnE[s], x_res[:, n, :], mv[:, s, 0:1], rstd[:, s:s + 1],
                                      ALU.subtract, ALU.mult).then_inc(sem("xnE"), 1)
                    dve.wait_ge(sem("xnE"), n + 1)
                    dve.tensor_tensor(x_res[:, n, :], x_res[:, n, :], gob, ALU.add).then_inc(sem("x3a"), 1)
                if back is not None:
                    n, s = back.n, back.slot
                    dve.wait_ge(sem("pv"), n + 1)
                    pv = bank[4][:, 0:H * (HD + 1)].rearrange("p (h d) -> p h d", h=H)
                    dve.reciprocal(rsum[s], pv[:, :, HD:HD + 1].rearrange("p h a -> p (h a)")).then_inc(sem("rsum"), 1)
                    dve.wait_ge(sem("rsum"), n + 1)
                    reach(dve, sem("oT_ps"), n - 1)
                    dve.tensor_tensor(oE[s], pv[:, :, 0:HD], rsum[s].unsqueeze(2).to_broadcast([P, H, HD]), ALU.mult)\
                        .then_inc(sem("oE"), 1)
                    dve.wait_ge(sem("o_ps"), n + 1)
                    dve.wait_ge(sem("x3a"), n + 1)
                    dve.scalar_tensor_tensor(x_res[:, n, :], bank[4][:, 0:D], tg[:, GX1:GX1 + 1], x_res[:, n, :],
                                             ALU.mult, ALU.add).then_inc(sem("x3"), 1)
            run_steps(dve, T, 2, 2, attn, lead=2)


            def ffn(at):
                i = at(0)
                if i is not None:
                    n, s = i.n, i.slot
                    wait_apart(dve, (sem("const"), 14), (sem("x3"), n + 1))
                    dve.bn_stats(stats[:, s, :], x_res[:, n, :]).then_inc(sem("stF"), 1)
                    wait_apart(dve, (sem("const"), 14), (sem("stF"), n + 1))
                    dve.bn_aggr(mv[:, s, :], stats[:, s, :]).then_inc(sem("mvF"), 1)
                i = at(1)
                if i is not None:
                    n, s = i.n, i.slot
                    dve.wait_ge(sem("rstdF"), n + 1)
                    dve.tensor_scalar(xnF[s], x_res[:, n, :], mv[:, s, 0:1], rstd[:, s:s + 1],
                                      ALU.subtract, ALU.mult).then_inc(sem("xnF"), 1)
                    wait_apart(dve, (sem("const"), 14), (sem("xnF"), n + 1))
                    quantise(xnF[s], D, amx, amc, arc, xyF, xeF, xaF, "quantx", 8 * n)
                    reach(dve, sem("xTF_ps"), n - 1)
                    rescale(xqF[s], xaF, amc).then_inc(sem("xqF"), 1)
                i = at(2)
                if i is not None:
                    n = i.n
                    for h in range(2):
                        dve.wait_ge(sem("sgF"), 2 * n + h + 1)
                        dve.wait_ge(sem("gu8"), 4 * n + 2 * h + 2)
                        reach(dve, sem("hqF"), 2 * n + h - 1)
                        dve.tensor_tensor(hF[h], bank[4 + h][:, :], sgF[h], ALU.mult).then_inc(sem("hF"), 1)
                        wait_apart(dve, (sem("const"), 14), (sem("hF"), 2 * n + h + 1))
                        quantise(hF[h], HW, amh[h], ahc[h], ahr[h], hyF, heF, haF[h], "quant",
                                 14 * n + 7 * h, last="hround")
                i = at(3)
                if i is not None:
                    n = i.n
                    dve.wait_ge(sem("dF"), n + 1)
                    dve.scalar_tensor_tensor(x_res[:, n, :], bank[1][:, 0:D], tg[:, GF1:GF1 + 1], x_res[:, n, :],
                                             ALU.mult, ALU.add).then_inc(sem("x4"), 1)
            run_steps(dve, T, 3, 2, ffn, lead=2)

        @block.tensor
        def _(pe):
            pe.wait_ge(sem("const"), 14)

            def turn(dst, src, m=P, k=P):
                return pe.transpose(dst, src, ident[0:k, 0:k])

            pe.wait_ge(sem("wnat_in"), 64)
            for n in range(8):
                w, c = n // 2, n % 2
                reach(pe, sem("wT"), n - 1)
                for o in range(2):
                    ins = turn(bank[6 + n % 2][:, o * P:(o + 1) * P], w_nat[:, w, o, c * P:(c + 1) * P])
                ins.then_inc(sem("wT_ps"), 1)

            def wkv_pe(at):
                i = at(0)
                if i is not None:
                    n, s = i.n, i.slot
                    pe.wait_ge(sem("xnA"), n + 1)
                    pe.wait_ge(sem(f"cxA_in{s}"), 16 * (i.lap + 1))
                    reach(pe, sem("exps"), n - 1)
                    reach(pe, sem("vTs"), n - 1)
                    for c in range(C):
                        turn(bank[s][:, c * P:(c + 1) * P], xnA[s][:, c * P:(c + 1) * P])
                        ins = turn(bank[2 + s][:, c * P:(c + 1) * P], cxA[s][:, c * P:(c + 1) * P])
                    ins.then_inc(sem("kvT"), 1)
                i = at(2)
                if i is not None:
                    n, s = i.n, i.slot
                    pe.wait_ge(sem("yA"), n + 1)
                    reach(pe, sem("x1"), n - 1)
                    for c in range(C):
                        ins = turn(bank[4 + s][:, c * P:(c + 1) * P], yA[s][:, c, :])
                    ins.then_inc(sem("yT_ps"), 1)
            run_steps(pe, T, 2, 2, wkv_pe, lead=2)

            def route_pe(at):
                i = at(0)
                if i is not None:
                    n, s = i.n, i.slot
                    pe.wait_ge(sem("h1"), n + 1)
                    reach(pe, sem("h1T"), n - 1)
                    for c in range(C):
                        ins = turn(bank[s][:, c * P:(c + 1) * P], h1B[s][:, c * P:(c + 1) * P])
                    ins.then_inc(sem("h1T_ps"), 1)
                    pe.wait_ge(sem("h1T"), n + 1)
                    reach(pe, sem("pexp"), n - 1)
                    reach(pe, sem("biased"), n - 1)
                    for c in range(C):
                        ins = pe.matmul(bank[2 + s][:, 0:E], h1Ts[s][:, c, :], router_sb[:, c, :],
                                        start=(c == 0), stop=(c == C - 1))
                    ins.then_inc(sem("logits"), 1)
                i = at(1)
                if i is not None:
                    n, s = i.n, i.slot
                    pe.wait_ge(sem("mask"), n + 1)
                    reach(pe, sem("macc"), n)
                    reach(pe, sem("ck"), n - 1)
                    pe.matmul(bank[4 + s][:, 0:E], tri[:, :], mask[s], start=True, stop=False)
                    pe.matmul(bank[4 + s][:, 0:E], ones[:, :], macc[:, s, :], start=False, stop=True)\
                        .then_inc(sem("rank"), 1)
            run_steps(pe, T, 1, 2, route_pe)
            pe.wait_ge(sem("macc"), T)
            pe.matmul(bank[6][:, 0:E], ones[:, :], macc[:, 0, :], start=True, stop=True).then_inc(sem("counts"), 1)

            pe.wait_ge(sem("shared_in"), 6 * 16)
            pe.wait_ge(sem("pexp"), T)
            pe.wait_ge(sem("h1T_all"), T)
            for n in range(8):
                f, hf = n % 4, n // 4
                reach(pe, sem("sgt"), n - 1)
                for part in range(2):
                    for c in range(C):
                        ins = pe.matmul(bank[2 * part + n % 2][:, :], sgu_w[:, c, part * SH + f * P:part * SH + (f + 1) * P],
                                        h1T[:, c, hf * 512:(hf + 1) * 512], start=(c == 0), stop=(c == C - 1))
                ins.then_inc(sem("sup_ps"), 1)
                if n == 3:
                    pe.wait_ge(sem("eidm"), 1)
                    pe.matmul(bank[7][0:1, 0:P], eidm, ident[:, :], start=True, stop=True).then_inc(sem("eid_ps"), 1)
            pe.wait_ge(sem("rc"), T)

            def table_pe(at):
                i = at(0)
                if i is None:
                    return
                pe.wait_ge(sem("onehots"), i.n + 1)
                first = isinstance(i.n, int) and i.n == 0
                last = isinstance(i.n, int) and i.n == T * K - 1
                pe.matmul(bank[5][:, 0:NB], poh[i.slot], boh[i.slot], start=first, stop=last)\
                    .then_inc(sem("tab_ps"), 1)
            run_steps(pe, T * K, 0, 4, table_pe, tail=4)
            pe.wait_ge(sem("sgt"), 8)
            pe.wait_ge(sem("hs"), 8)
            for t in range(T):
                reach(pe, sem("xs"), t - 1)
                for f in range(4):
                    ins = pe.matmul(bank[2 + t % 2][:, 0:D], hs[:, f, t * P:(t + 1) * P], sd_w[:, f, :],
                                    start=(f == 0), stop=(f == 3))
                ins.then_inc(sem("sdown"), 1)

            pe.wait_ge(sem("moe_in"), 16 * 18)
            pe.wait_ge(sem("moe_in2"), 16 * 2)
            pe.wait_ge(sem("eid"), 1)
            pe.wait_ge(sem("tok"), 1)
            pe.wait_ge(sem("xs"), T)

            def experts_of(group):
                _, values = nc.values_load_multi_w_load_instructions(
                    eid_row[0:1, bass.ds(4 * group, 4)], engines=[mybir.EngineType.PE], min_val=0, max_val=E - 1,
                    skip_runtime_bounds_check_because="eidm is a count of experts, clamped to E - 1")
                return values

            def moe_pe(at):
                i, nxt = at(1), at(0)

                def turn_tokens(p):
                    if nxt is None:
                        return
                    pair, slot = 2 * nxt.n + p, 2 * nxt.slot + p
                    pe.wait_ge(sem(f"xg{slot}"), 32 * (nxt.lap + 1))
                    reach(pe, sem("xgT"), pair - 1)
                    for b in range(2):
                        for c in range(C):
                            ins = turn(bank[p][:, (2 * b + c) * P:(2 * b + c + 1) * P],
                                       xg[slot][:, b, c * P:(c + 1) * P])
                    ins.then_inc(sem("xgT_ps"), 1)

                if i is None:
                    turn_tokens(0)
                    turn_tokens(1)
                    return
                experts = experts_of(i.n)
                for p in range(2):
                    pe.wait_ge(sem("xgT"), 2 * i.n + p + 1)
                    reach(pe, sem("hb"), 2 * i.n + p - 1)
                    for b in range(2):
                        for c in range(C):
                            ins = pe.matmul(bank[2 + p][:, 2 * F * b:2 * F * (b + 1)], xgT[p][:, b, c, :],
                                            moe_up[:, c, bass.ds(experts[2 * p + b], 1), :].rearrange("p a f -> p (a f)"),
                                            start=(c == 0), stop=(c == C - 1))
                    ins.then_inc(sem("gu"), 1)
                for p in range(2):
                    turn_tokens(p)
                    wait_apart(pe, (sem("tok"), 1), (sem("hb"), 2 * i.n + p + 1), (sem("hbT"), 2 * i.n + p - 1))
                    for b in range(2):
                        ins = turn(bank[4 + p][0:F, b * P:(b + 1) * P], hb[p][:, b, :])
                    ins.then_inc(sem("hT_ps"), 1)
                for p in range(2):
                    pe.wait_ge(sem("hbT"), 2 * i.n + p + 1)
                    reach(pe, sem("ysb"), 2 * i.n + p - 1)
                    for b in range(2):
                        ins = pe.matmul(bank[6 + p][:, b * D:(b + 1) * D], hbT[p][0:F, b, :],
                                        moe_dn[:, bass.ds(experts[2 * p + b], 1), :].rearrange("p a d -> p (a d)"),
                                        start=True, stop=True)
                    ins.then_inc(sem("mo_y"), 1)
            run_steps(pe, NB // 4, 1, 2, moe_pe)
            pe.wait_ge(sem("ysb"), NB // 2)

            def upto(v):
                return min(v, T) if isinstance(v, int) else v

            def mx_turns():
                for n in range(12):
                    pe.wait_ge(sem("w_deq"), 2 * n + 2)
                    reach(pe, sem("mxT"), n - 1)
                    for k in range(4):
                        ins = turn(bank[6 + n % 2][:, k * P:(k + 1) * P], mx_w[:, n * 512 + k * P:n * 512 + (k + 1) * P])
                    ins.then_inc(sem("mxT_ps"), 1)
                pe.wait_ge(sem("mxT"), 12)

            def attn_pe(at):
                front, mid, back = at(0), at(1), at(2)
                if back is not None:
                    n, s = back.n, back.slot
                    pe.wait_ge(sem("qT"), n + 1)
                    pe.wait_ge(sem("kT"), n + 1)
                    pe.wait_ge(sem("xTE"), upto(n + 2))
                    for j in range(4):
                        rows = slice(HP * j, HP * j + HP)
                        for g in range(4):
                            ins = pe.matmul(bank[j][:, g * P:(g + 1) * P], qT[s][rows, g, :], kT[s][rows, g, :],
                                            start=True, stop=True)
                        ins.then_inc(sem("S"), 1)
                if mid is not None:
                    n, s = mid.n, mid.slot
                    pe.wait_ge(sem("cTE"), n + 1)
                    reach(pe, sem("x3"), n - 1)
                    for w in (1, 2):
                        for c in range(C):
                            ins = pe.matmul(bank[4][:, (w - 1) * D:w * D], cTE[s][:, c, :], attn_w[:, w, c, :],
                                            start=(c == 0), stop=(c == C - 1))
                    ins.then_inc(sem("kv_ps"), 1)
                    pe.wait_ge(sem("xTE"), n + 1)
                    reach(pe, sem("oT"), n - 1)
                    for c in range(C):
                        ins = pe.matmul(bank[5][:, 0:D], xTE[s][:, c, :], attn_w[:, 0, c, :],
                                        start=(c == 0), stop=(c == C - 1))
                    ins.then_inc(sem("q_ps"), 1)
                    if back is None:
                        mx_turns()
                if back is not None:
                    n, s = back.n, back.slot
                    for j in range(4):
                        pe.wait_ge(sem("probs"), 4 * n + j + 1)
                        reach(pe, sem("pT"), 4 * n + j - 1)
                        for g in range(4):
                            ins = turn(bank[6 + j % 2][:, g * P:(g + 1) * P], sS[:, j, g, :])
                        ins.then_inc(sem("pT_ps"), 1)
                    pe.wait_ge(sem("va"), upto(n + 2))
                    for j in range(4):
                        pe.wait_ge(sem("pT"), 4 * n + j + 1)
                        for g in range(4):
                            h = 4 * g + j
                            ins = pe.matmul(bank[4][:, h * (HD + 1):(h + 1) * (HD + 1)], pT[:, j, g, :],
                                            va[s][:, h, :], start=True, stop=True)
                    ins.then_inc(sem("pv"), 1)
                if mid is not None:
                    n, s = mid.n, mid.slot
                    for name, src, b in (("q", qn, 1), ("k", kn, 0)):
                        pe.wait_ge(sem(f"{name}n"), n + 1)
                        for g in range(4):
                            ins = turn(bank[b][:, g * P:(g + 1) * P],
                                       src[s][:, 4 * g:4 * g + 4, :].rearrange("p h d -> p (h d)"))
                        ins.then_inc(sem(f"{name}T_ps"), 1)
                if back is not None:
                    n, s = back.n, back.slot
                    pe.wait_ge(sem("oE"), n + 1)
                    for c in range(C):
                        ins = turn(bank[5][:, c * P:(c + 1) * P],
                                   oE[s].rearrange("p h d -> p (h d)")[:, c * P:(c + 1) * P])
                    ins.then_inc(sem("oT_ps"), 1)
                if front is not None:
                    n, s = front.n, front.slot
                    pe.wait_ge(sem(f"cxE_in{s}"), 16 * (front.lap + 1))
                    for c in range(C):
                        ins = turn(bank[2][:, c * P:(c + 1) * P], cxE[s][:, c * P:(c + 1) * P])
                    ins.then_inc(sem("cTE_ps"), 1)
                    pe.wait_ge(sem("xnE"), n + 1)
                    for c in range(C):
                        ins = turn(bank[3][:, c * P:(c + 1) * P], xnE[s][:, c * P:(c + 1) * P])
                    ins.then_inc(sem("xTE_ps"), 1)
                if back is not None:
                    n, s = back.n, back.slot
                    pe.wait_ge(sem("oT"), n + 1)
                    for c in range(C):
                        ins = pe.matmul(bank[4][:, 0:D], oT[s][:, c, :], attn_w[:, 3, c, :],
                                        start=(c == 0), stop=(c == C - 1))
                    ins.then_inc(sem("o_ps"), 1)
            run_steps(pe, T, 2, 2, attn_pe, lead=2)
            pe.wait_ge(sem("x3"), T)

            def ffn_pe(at):
                i = at(0)
                if i is not None:
                    n, s = i.n, i.slot
                    pe.wait_ge(sem("xqF"), n + 1)
                    for c in range(C):
                        ins = turn(bank[0][:, c * P:(c + 1) * P], xqF[s][:, c * P:(c + 1) * P])
                    ins.then_inc(sem("xTF_ps"), 1)
                    pe.wait_ge(sem("xTF"), n + 1)
                    for h in range(2):
                        reach(pe, sem("hF"), 2 * n + h - 1)
                        for part in range(2):
                            lo = part * INNER + h * HW
                            for c in range(C):
                                ins = pe.matmul(bank[2 + 2 * part + h][:, :], xTF[s][:, c, :], mx_gu[:, c, lo:lo + HW],
                                                start=(c == 0), stop=(c == C - 1))
                            ins.then_inc(sem("gu8"), 1)
                i = at(1)
                if i is not None:
                    n, s = i.n, i.slot
                    for h in range(2):
                        pe.wait_ge(sem("hqF"), 2 * n + h + 1)
                        reach(pe, sem("hTF"), 2 * n + h - 1)
                        for k in range(4):
                            ins = turn(bank[6 + h][:, k * P:(k + 1) * P], hqF[s][:, h * HW + k * P:h * HW + (k + 1) * P])
                        ins.then_inc(sem("hTF_ps"), 1)
                    reach(pe, sem("x4"), n)
                    for k in range(8):
                        if k % 4 == 0:
                            pe.wait_ge(sem("hTF"), 2 * n + 1 + k // 4)
                        ins = pe.matmul(bank[1][:, 0:D], hTF[s][:, k, :], mx_dn[:, k, :], start=(k == 0), stop=(k == 7))
                    ins.then_inc(sem("dF"), 1)
            run_steps(pe, T, 1, 2, ffn_pe)


_INS = ['x', 'ctx_2048', 'g_xattn', 'g_ffn', 'L0_xattn_time_decay', 'L0_xattn_time_first',
        'L0_ffn_router_w', 'L0_ffn_router_bias', 'L0_ffn_wg', 'L0_ffn_wu', 'L0_ffn_wd', 'L0_ffn_swg',
        'L0_ffn_swu', 'L0_ffn_swd', 'L1_xattn_q_w', 'L1_xattn_q_b', 'L1_xattn_k_img_w',
        'L1_xattn_k_img_b', 'L1_xattn_v_img_w', 'L1_xattn_v_img_b', 'L1_xattn_o_w', 'L1_xattn_o_b',
        'L1_xattn_norm_q_w', 'L1_xattn_norm_k_img_w', 'L1_ffn_gate_w', 'L1_ffn_up_w', 'L1_ffn_down_w']


def kernel(**inputs):
    import numpy as _np
    import concourse.bacc as _bacc
    from concourse import mybir as _mybir
    from concourse.bass_utils import run_bass_kernel_spmd as _run

    nc = _bacc.Bacc("TRN2", target_bir_lowering=False, num_devices=1)
    arrays, args = {}, []
    for name in _INS:
        a = _np.ascontiguousarray(inputs[name])
        arrays[f"in_{name}_dram"] = a
        args.append(nc.dram_tensor(f"in_{name}_dram", a.shape, _mybir.dt.from_np(a.dtype), kind="ExternalInput").ap())
    out = nc.dram_tensor("out_dram", (T, P, D), F32, kind="ExternalOutput").ap()
    build_program(nc, *args, out)
    r = _run(nc, [arrays], core_ids=[0])
    return r.results[0]["out_dram"]
```
